# Optimizing a Trainium2 kernel written in Bass

```python
import numpy as np
import jax
import jax.numpy as jnp

def _softmax(x, axis=-1):
    return jax.nn.softmax(x, axis=axis)

def _gelu(x):
    return jax.nn.gelu(x, approximate=True)

def _silu(x):
    return jax.nn.silu(x)

def _sigmoid(x):
    return jax.nn.sigmoid(x)

def _layernorm(x, axis=-1, eps=1e-05):
    m = jnp.mean(x, axis=axis, keepdims=True)
    v = jnp.var(x, axis=axis, keepdims=True)
    return (x - m) / jnp.sqrt(v + eps)

def _scatter_add(tgt, idx, src, axis=0):
    return tgt.at[idx].add(src)

def _segment_sum(src, seg, n):
    return jax.ops.segment_sum(src, seg, n)
kernel_name = 'mk_xattn_ffn_d2_seqx_r8_a454be'

def setup_inputs(seed: int=0):
    np.random.seed(seed)
    _w = jnp.asarray

    def _rec_inputs():
        import jax
        import jax.numpy as jnp
        _rk = jax.random.key(seed)
        x = -0.0005207 + 1.001 * jax.random.normal(jax.random.fold_in(_rk, 1), (32, 128, 128), jnp.float32)
        _lenS = 128 - jax.random.randint(jax.random.fold_in(_rk, 7), (32,), 0, max(1, 128 // 4) + 1, jnp.int32)
        _lenS2 = 128 - jax.random.randint(jax.random.fold_in(_rk, 8), (32,), 0, max(1, 128 // 4) + 1, jnp.int32)
        _ctx_1024P = jax.random.normal(jax.random.fold_in(_rk, 11), (32, 16, 128), jnp.float32)
        _ctx_1024c = jax.random.dirichlet(jax.random.fold_in(_rk, 511), 0.3 * jnp.ones((16,), jnp.float32), (32, 128))
        _ctx_1024t = jnp.einsum('bsk,bkd->bsd', _ctx_1024c, _ctx_1024P)
        _ctx_1024t = _ctx_1024t * jax.lax.rsqrt(jnp.mean(jnp.square(_ctx_1024t)) + 1e-12) * 0.953939
        ctx_1024 = -0.000514642 + 1.00011 * (_ctx_1024t + 0.3 * jax.random.normal(jax.random.fold_in(_rk, 611), (32, 128, 128), jnp.float32))
        return (x, ctx_1024)
    x, ctx_1024 = _rec_inputs()

    def _L0_xattn_setup():
        import jax, jax.numpy as jnp
        import numpy as np
        D_MODEL = 128
        FFN = 512
        E = 8
        K = 2
        B, S = (4, 64)
        key = jax.random.key(seed)
        ks = jax.random.split(key, 8)
        scale_in = 1.0 / np.sqrt(D_MODEL)
        scale_ffn = 1.0 / np.sqrt(FFN)
        return {'x': jax.random.normal(ks[0], (B, S, D_MODEL), jnp.float32), 'context': jax.random.normal(ks[1], (B, S, D_MODEL), jnp.float32), 'Wg': jax.random.normal(ks[2], (D_MODEL, E), jnp.float32) * scale_in, 'bg': jnp.zeros((E,), jnp.float32), 'W1': jax.random.normal(ks[3], (E, D_MODEL, FFN), jnp.float32) * scale_in, 'b1': jnp.zeros((E, FFN), jnp.float32), 'W2': jax.random.normal(ks[4], (E, FFN, D_MODEL), jnp.float32) * scale_ffn, 'b2': jnp.zeros((E, D_MODEL), jnp.float32)}
    _L0_xattn_all = _L0_xattn_setup()
    _L0_xattn_in = {k: v for k, v in _L0_xattn_all.items() if k in ('Wg', 'bg', 'W1', 'b1', 'W2', 'b2')}
    del _L0_xattn_all

    def _L0_ffn_setup():
        import jax, jax.numpy as jnp
        import numpy as np
        TOPK = 4
        N_GROUPS = 4
        TOPK_GROUPS = 2
        ROUTE_SCALE = 2.5

        def _gate(x2, Wg):
            T = x2.shape[0]
            E = Wg.shape[0]
            scores = x2 @ Wg.T
            s = jax.nn.sigmoid(scores)
            g = s.reshape(T, N_GROUPS, E // N_GROUPS)
            group_scores = g.max(axis=-1)
            _, gidx = jax.lax.top_k(group_scores, TOPK_GROUPS)
            group_mask = jnp.any(jax.nn.one_hot(gidx, N_GROUPS, dtype=jnp.bool_), axis=1)
            masked = jnp.where(group_mask[:, :, None], g, -jnp.inf).reshape(T, E)
            _, idx = jax.lax.top_k(masked, TOPK)
            w = jnp.take_along_axis(s, idx, axis=1)
            w = w / jnp.sum(w, axis=-1, keepdims=True)
            w = w * ROUTE_SCALE
            return (w.astype(x2.dtype), idx)
        key = jax.random.key(seed)
        ks = jax.random.split(key, 6)
        B, S, D, I, E = (2, 256, 128, 128, 16)
        scale = 0.02
        return {'x': jax.random.normal(ks[0], (B, S, D), dtype=jnp.float32), 'Wg': jax.random.normal(ks[1], (E, D), dtype=jnp.float32) * scale, 'W1': jax.random.normal(ks[2], (E, I, D), dtype=jnp.float32) * scale, 'b1': jnp.zeros((E, I), dtype=jnp.float32), 'W2': jax.random.normal(ks[3], (E, D, I), dtype=jnp.float32) * scale, 'b2': jnp.zeros((E, D), dtype=jnp.float32), 'W3': jax.random.normal(ks[4], (E, I, D), dtype=jnp.float32) * scale, 'b3': jnp.zeros((E, I), dtype=jnp.float32)}
    _L0_ffn_all = _L0_ffn_setup()
    _L0_ffn_in = {k: v for k, v in _L0_ffn_all.items() if k in ('Wg', 'W1', 'b1', 'W2', 'b2', 'W3', 'b3')}
    del _L0_ffn_all

    def _L1_xattn_setup():
        import jax, jax.numpy as jnp
        import numpy as np
        EMBED_PHI = 128
        EMBED_F = 128
        HIDDEN_F = 128
        N_HEADS = 16
        B, S = (2, 256)
        key = jax.random.key(seed)
        ks = jax.random.split(key, 9)
        sphi = 1.0 / np.sqrt(EMBED_PHI)
        sf = 1.0 / np.sqrt(EMBED_F)
        sh = 1.0 / np.sqrt(HIDDEN_F)
        return {'q': jax.random.normal(ks[0], (B, S, EMBED_PHI), jnp.float32), 'k': jax.random.normal(ks[1], (B, S, EMBED_PHI), jnp.float32), 'v': jax.random.normal(ks[2], (B, S, EMBED_F), jnp.float32), 'Wq': jax.random.normal(ks[3], (HIDDEN_F, EMBED_PHI), jnp.float32) * sphi, 'Wk': jax.random.normal(ks[4], (HIDDEN_F, EMBED_PHI), jnp.float32) * sphi, 'Wv': jax.random.normal(ks[5], (HIDDEN_F, EMBED_F), jnp.float32) * sf, 'bv': jax.random.normal(ks[6], (HIDDEN_F,), jnp.float32) * sf, 'Wo': jax.random.normal(ks[7], (EMBED_F, HIDDEN_F), jnp.float32) * sh, 'bo': jax.random.normal(ks[8], (EMBED_F,), jnp.float32) * sh}
    _L1_xattn_all = _L1_xattn_setup()
    _L1_xattn_in = {k: v for k, v in _L1_xattn_all.items() if k in ('Wq', 'Wk', 'Wv', 'bv', 'Wo', 'bo')}
    del _L1_xattn_all

    def _L1_ffn_setup():
        import jax, jax.numpy as jnp
        import numpy as np
        B, S, H, F, G = (8, 256, 128, 512, 128)
        EPS = 1e-05

        def _dequant(q, scales, g):
            K, N = q.shape
            w = (q.astype(jnp.float32) - 128.0).reshape(K // g, g, N) * scales[:, None, :]
            return w.reshape(K, N)
        key = jax.random.key(seed)
        ks = jax.random.split(key, 8)
        x = jax.random.normal(ks[0], (B, S, H), dtype=jnp.float32)
        ln_gamma = jnp.ones((H,), jnp.float32)
        ln_beta = jnp.zeros((H,), jnp.float32)
        fc1_q = jax.random.randint(ks[1], (H, F), 0, 32, dtype=jnp.int32)
        fc2_q = jax.random.randint(ks[2], (F, H), 0, 32, dtype=jnp.int32)
        fc1_scales = jax.random.uniform(ks[3], (H // G, F), jnp.float32) * 0.02 + 0.001
        fc2_scales = jax.random.uniform(ks[4], (F // G, H), jnp.float32) * 0.02 + 0.001
        fc1_bias = jax.random.normal(ks[5], (F,), jnp.float32) * 0.02
        fc2_bias = jax.random.normal(ks[6], (H,), jnp.float32) * 0.02
        return {'x': x, 'ln_gamma': ln_gamma, 'ln_beta': ln_beta, 'fc1_q': fc1_q, 'fc1_scales': fc1_scales, 'fc1_bias': fc1_bias, 'fc2_q': fc2_q, 'fc2_scales': fc2_scales, 'fc2_bias': fc2_bias}
    _L1_ffn_all = _L1_ffn_setup()
    _L1_ffn_in = {k: v for k, v in _L1_ffn_all.items() if k in ('ln_gamma', 'ln_beta', 'fc1_q', 'fc1_scales', 'fc1_bias', 'fc2_q', 'fc2_scales', 'fc2_bias')}
    del _L1_ffn_all
    return {'x': x, 'ctx_1024': ctx_1024, 'L0_xattn_Wg': _L0_xattn_in['Wg'], 'L0_xattn_bg': _L0_xattn_in['bg'], 'L0_xattn_W1': _L0_xattn_in['W1'], 'L0_xattn_b1': _L0_xattn_in['b1'], 'L0_xattn_W2': _L0_xattn_in['W2'], 'L0_xattn_b2': _L0_xattn_in['b2'], 'L0_ffn_Wg': _L0_ffn_in['Wg'], 'L0_ffn_W1': _L0_ffn_in['W1'], 'L0_ffn_b1': _L0_ffn_in['b1'], 'L0_ffn_W2': _L0_ffn_in['W2'], 'L0_ffn_b2': _L0_ffn_in['b2'], 'L0_ffn_W3': _L0_ffn_in['W3'], 'L0_ffn_b3': _L0_ffn_in['b3'], 'L1_xattn_Wq': _L1_xattn_in['Wq'], 'L1_xattn_Wk': _L1_xattn_in['Wk'], 'L1_xattn_Wv': _L1_xattn_in['Wv'], 'L1_xattn_bv': _L1_xattn_in['bv'], 'L1_xattn_Wo': _L1_xattn_in['Wo'], 'L1_xattn_bo': _L1_xattn_in['bo'], 'L1_ffn_ln_gamma': _L1_ffn_in['ln_gamma'], 'L1_ffn_ln_beta': _L1_ffn_in['ln_beta'], 'L1_ffn_fc1_q': _L1_ffn_in['fc1_q'], 'L1_ffn_fc1_scales': _L1_ffn_in['fc1_scales'], 'L1_ffn_fc1_bias': _L1_ffn_in['fc1_bias'], 'L1_ffn_fc2_q': _L1_ffn_in['fc2_q'], 'L1_ffn_fc2_scales': _L1_ffn_in['fc2_scales'], 'L1_ffn_fc2_bias': _L1_ffn_in['fc2_bias']}

def reference(x, ctx_1024, L0_xattn_Wg, L0_xattn_bg, L0_xattn_W1, L0_xattn_b1, L0_xattn_W2, L0_xattn_b2, L0_ffn_Wg, L0_ffn_W1, L0_ffn_b1, L0_ffn_W2, L0_ffn_b2, L0_ffn_W3, L0_ffn_b3, L1_xattn_Wq, L1_xattn_Wk, L1_xattn_Wv, L1_xattn_bv, L1_xattn_Wo, L1_xattn_bo, L1_ffn_ln_gamma, L1_ffn_ln_beta, L1_ffn_fc1_q, L1_ffn_fc1_scales, L1_ffn_fc1_bias, L1_ffn_fc2_q, L1_ffn_fc2_scales, L1_ffn_fc2_bias):
    import jax
    import jax.numpy as jnp

    def _L0_xattn_ref(x, context, Wg, bg, W1, b1, W2, b2):
        import jax, jax.numpy as jnp
        import numpy as np
        D_MODEL = 128
        FFN = 512
        E = 8
        K = 2
        B, S = (4, 64)
        logits = jnp.einsum('bsd,de->bse', context, Wg) + bg
        scores_topk, idx_topk = jax.lax.top_k(logits, K)
        weights = jax.nn.softmax(scores_topk, axis=-1)
        combine = jnp.sum(jax.nn.one_hot(idx_topk, E, dtype=weights.dtype) * weights[..., None], axis=-2)
        h = jax.nn.relu(jnp.einsum('bsd,edf->bsef', x, W1) + b1)
        y = jnp.einsum('bsef,efd->bsed', h, W2) + b2
        out = jnp.einsum('bsed,bse->bsd', y, combine)
        return out

    def _L0_ffn_ref(x, Wg, W1, b1, W2, b2, W3, b3):
        import jax, jax.numpy as jnp
        import numpy as np
        TOPK = 4
        N_GROUPS = 4
        TOPK_GROUPS = 2
        ROUTE_SCALE = 2.5

        def _gate(x2, Wg):
            T = x2.shape[0]
            E = Wg.shape[0]
            scores = x2 @ Wg.T
            s = jax.nn.sigmoid(scores)
            g = s.reshape(T, N_GROUPS, E // N_GROUPS)
            group_scores = g.max(axis=-1)
            _, gidx = jax.lax.top_k(group_scores, TOPK_GROUPS)
            group_mask = jnp.any(jax.nn.one_hot(gidx, N_GROUPS, dtype=jnp.bool_), axis=1)
            masked = jnp.where(group_mask[:, :, None], g, -jnp.inf).reshape(T, E)
            _, idx = jax.lax.top_k(masked, TOPK)
            w = jnp.take_along_axis(s, idx, axis=1)
            w = w / jnp.sum(w, axis=-1, keepdims=True)
            w = w * ROUTE_SCALE
            return (w.astype(x2.dtype), idx)
        shape = x.shape
        D = shape[-1]
        x2 = x.reshape(-1, D)
        weights, indices = _gate(x2, Wg)
        E = Wg.shape[0]
        y = jnp.zeros_like(x2)
        for e in range(E):
            we = jnp.sum(weights * (indices == e), axis=-1)
            h = jax.nn.silu(x2 @ W1[e].T + b1[e]) * (x2 @ W3[e].T + b3[e])
            y = y + (h @ W2[e].T + b2[e]) * we[:, None]
        return y.reshape(shape)

    def _L1_xattn_ref(q, k, v, Wq, Wk, Wv, bv, Wo, bo):
        import jax, jax.numpy as jnp
        import numpy as np
        EMBED_PHI = 128
        EMBED_F = 128
        HIDDEN_F = 128
        N_HEADS = 16
        B, S = (2, 256)
        Bq, Sq, _ = q.shape
        hd = HIDDEN_F // N_HEADS
        scale = 1.0 / np.sqrt(hd)
        qh = (q @ Wq.T).reshape(Bq, Sq, N_HEADS, hd).transpose(0, 2, 1, 3)
        kh = (k @ Wk.T).reshape(Bq, Sq, N_HEADS, hd).transpose(0, 2, 1, 3)
        vh = (v @ Wv.T + bv).reshape(Bq, Sq, N_HEADS, hd).transpose(0, 2, 1, 3)
        scores = jnp.einsum('bhsd,bhtd->bhst', qh, kh) * scale
        mask = jnp.triu(jnp.ones((Sq, Sq), dtype=bool), k=0).at[0, 0].set(False)
        scores = jnp.where(mask, -jnp.inf, scores)
        probs = jax.nn.softmax(scores, axis=-1)
        out = jnp.einsum('bhst,bhtd->bhsd', probs, vh)
        out = out.transpose(0, 2, 1, 3).reshape(Bq, Sq, HIDDEN_F)
        return out @ Wo.T + bo

    def _L1_ffn_ref(x, ln_gamma, ln_beta, fc1_q, fc1_scales, fc1_bias, fc2_q, fc2_scales, fc2_bias):
        import jax, jax.numpy as jnp
        import numpy as np
        B, S, H, F, G = (8, 256, 128, 512, 128)
        EPS = 1e-05

        def _dequant(q, scales, g):
            K, N = q.shape
            w = (q.astype(jnp.float32) - 128.0).reshape(K // g, g, N) * scales[:, None, :]
            return w.reshape(K, N)
        residual = x
        mu = jnp.mean(x, axis=-1, keepdims=True)
        var = jnp.mean(jnp.square(x - mu), axis=-1, keepdims=True)
        h = (x - mu) * jax.lax.rsqrt(var + EPS) * ln_gamma + ln_beta
        hf = h.reshape(-1, H)
        w1 = _dequant(fc1_q, fc1_scales, G)
        y = hf @ w1 + fc1_bias
        y = jax.nn.silu(y)
        w2 = _dequant(fc2_q, fc2_scales, G)
        z = y @ w2 + fc2_bias
        return residual + 0.5 * z.reshape(residual.shape)
    x = x + _L0_xattn_ref(_layernorm(x, axis=-1), ctx_1024, L0_xattn_Wg, L0_xattn_bg, L0_xattn_W1, L0_xattn_b1, L0_xattn_W2, L0_xattn_b2)
    x = x + _L0_ffn_ref(_layernorm(x, axis=-1), L0_ffn_Wg, L0_ffn_W1, L0_ffn_b1, L0_ffn_W2, L0_ffn_b2, L0_ffn_W3, L0_ffn_b3)
    x = x + _L1_xattn_ref(_layernorm(x, axis=-1), ctx_1024, ctx_1024, L1_xattn_Wq, L1_xattn_Wk, L1_xattn_Wv, L1_xattn_bv, L1_xattn_Wo, L1_xattn_bo)
    x = x + _L1_ffn_ref(_layernorm(x, axis=-1), L1_ffn_ln_gamma, L1_ffn_ln_beta, L1_ffn_fc1_q, L1_ffn_fc1_scales, L1_ffn_fc1_bias, L1_ffn_fc2_q, L1_ffn_fc2_scales, L1_ffn_fc2_bias)
    return x

_drawn_inputs = setup_inputs


def setup_inputs(seed=0):
    import zlib

    import numpy as np

    out = dict(_drawn_inputs(seed))
    spreads = {'L0_xattn_bg': (0.0, 0.1),
     'L0_xattn_b1': (0.0, 0.1),
     'L0_xattn_b2': (0.0, 0.1),
     'L0_ffn_b1': (0.0, 0.8),
     'L0_ffn_b2': (0.0, 0.523),
     'L0_ffn_b3': (0.0, 0.8),
     'L1_ffn_ln_gamma': (1.0, 0.2),
     'L1_ffn_ln_beta': (0.0, 0.1)}
    factors = {'L0_ffn_W1': 8.0,
     'L0_ffn_W2': 8.0,
     'L0_ffn_W3': 8.0,
     'L1_ffn_fc1_scales': 17.261,
     'L1_ffn_fc1_bias': 64.0,
     'L1_ffn_fc2_bias': 64.0,
     'L1_xattn_bv': 5.995,
     'L1_xattn_bo': 3.242}
    for name, (base, spread) in spreads.items():
        noise = np.random.default_rng([zlib.crc32(name.encode()), seed]).standard_normal(out[name].shape)
        drawn = base * np.exp(spread * noise) if base else spread * noise
        out[name] = jnp.asarray(drawn.astype(out[name].dtype))
    for name, factor in factors.items():
        out[name] = (out[name] * factor).astype(out[name].dtype)
    return out
```

```python
import numpy as np
import concourse.bass as bass
from concourse import mybir
from contextlib import ExitStack

F32 = mybir.dt.float32
F32R = mybir.dt.float32r
BF16 = mybir.dt.bfloat16
I32 = mybir.dt.int32
ALU = mybir.AluOpType
ACT = mybir.ActivationFunctionType
AX = mybir.AxisListType.X

P = 128
NB = 8
BT = 512
NT = BT // P
EPS = 1e-5

EA, FA = 8, 512
CA = FA // P
UA = EA * CA
EB = 16
NG = 4
CD = 4
ROUTE_SCALE = 2.5

NH, HD = 16, 8
HG = 4
SG = NH // HG
MASKED = -1e30

STAGE_A, STAGE_B, STAGE_C, STAGE_D = range(4)


def build(nc, x, ctxT, a_wg, a_bg, a_w1, a_b1, a_w2, a_b2,
          b_wg, b_w1, b_b1, b_w3, b_b3, b_w2, b_b2,
          c_wqk, c_wvo, c_sign, c_bv, c_bo, d_fc1, d_fc2, d_scales, d_gamma, d_beta, d_b1, d_b2, out):
    with ExitStack() as ctx:
        def sb(name, shape, dt=F32):
            return ctx.enter_context(nc.sbuf_tensor(name, shape, dt))

        def sem(name):
            return ctx.enter_context(nc.semaphore(name))

        hid_ps = [ctx.enter_context(nc.psum_tensor(f"hid_ps{k}", [P, BT], F32)) for k in range(4)]
        y_ps = [ctx.enter_context(nc.psum_tensor(f"y_ps{k}", [P, BT], F32)) for k in range(2)]
        cb_ps = ctx.enter_context(nc.psum_tensor("cb_ps", [P, BT], F32))
        tr_ps = ctx.enter_context(nc.psum_tensor("tr_ps", [P, BT], F32))

        X = sb("X", [P, NB * BT])
        xn = sb("xn", [P, BT])
        xTh = sb("xTh", [P, 2, BT], F32R)
        xTl = sb("xTl", [P, 2, BT], F32R)
        accT = sb("accT", [P, 2, BT])
        ident = sb("ident", [P, P])
        st = sb("st", [P, NT, 6])
        mv = sb("mv", [P, NT, 2])
        carry = sb("carry", [P, 1])
        veps = sb("veps", [P, NT])
        rstd = sb("rstd", [P, NT])
        mhalf = sb("mhalf", [P, NT])

        region1 = sb("region1", [P, 4 * EA * FA], F32R)
        region2 = sb("region2", [P, 4 * EB * P], F32R)

        def part(region, k, n, *dims):
            v = region[:, k * n:(k + 1) * n]
            if len(dims) < 2:
                return v
            names = [f"d{q}" for q in range(len(dims))]
            return v.rearrange(f"p ({' '.join(names)}) -> p {' '.join(names)}", **dict(zip(names, dims)))

        w1h, w1l = part(region1, 0, EA * FA, EA, FA), part(region1, 1, EA * FA, EA, FA)
        w2h, w2l = part(region1, 2, EA * FA, EA, CA, P), part(region1, 3, EA * FA, EA, CA, P)
        bw1h, bw1l = part(region2, 0, EB * P, EB, P), part(region2, 1, EB * P, EB, P)
        bw3h, bw3l = part(region2, 2, EB * P, EB, P), part(region2, 3, EB * P, EB, P)
        bw2h, bw2l = part(region1, 6, EB * P, EB, P), part(region1, 7, EB * P, EB, P)
        kdiag = [part(region1, k, NT * BT, NT, BT) for k in range(2)]
        qdiag = [part(region1, 2 + k, NT * BT, NT, BT) for k in range(2)]
        kp = part(region1, 4, 4 * BT, 4, BT)
        wqkh, wqkl = part(region2, 0, 2 * BT, 2, SG, P), part(region2, 1, 2 * BT, 2, SG, P)
        wvoh, wvol = part(region2, 10, 2 * P, 2, P), part(region2, 11, 2 * P, 2, P)
        fc1h, fc1l = part(region2, 6, BT), part(region2, 7, BT)
        fc2h, fc2l = part(region2, 8, BT, CD, P), part(region2, 9, BT, CD, P)
        raw = sb("raw", [P, 4, BT])

        hf = sb("hf", [P, 2, BT])
        hh = sb("hh", [P, 4, BT], F32R)
        hl = sb("hl", [P, 4, BT], F32R)
        wy = sb("wy", [P, 2, BT])
        cbs = sb("cbs", [P, 2, BT])
        sg = sb("sg", [P, 2, BT])
        combT = sb("combT", [2 * EB, 2, BT], F32R)
        sel = sb("sel", [2 * EB, EB, P], F32R)
        b1a, b2a = sb("b1a", [P, EA * CA]), sb("b2a", [P, EA])
        wga, bga = sb("wga", [P, EA]), sb("bga", [P, EA])
        b1b, b3b, b2b = sb("b1b", [P, EB]), sb("b3b", [P, EB]), sb("b2b", [P, EB])
        wgb = sb("wgb", [P, EB])
        wgbh, wgbl = sb("wgbh", [P, EB], F32R), sb("wgbl", [P, EB], F32R)
        ctxr = sb("ctxr", [P, 2, BT])
        TA = NB * NT
        TH = TA // 2
        lga = sb("lga", [P, TA, EA])
        combA = sb("combA", [P, TA, 2 * EA])
        lower = sb("lower", [P, EB, EB], BF16)
        upper = sb("upper", [P, EB, EB], BF16)
        rk1 = sb("rk1", [P, NT * EB * EB], BF16)
        rk2 = sb("rk2", [P, NT * EB * EB], BF16)
        rank = sb("rank", [P, TA, EA])
        mx = sb("mx", [P, TA])
        ex = sb("ex", [P, TA, EA])
        ssum = sb("ssum", [P, TA])
        hi32 = sb("hi32", [P, TA, EA], F32R)
        sgm = sb("sgm", [P, NT, EB])
        gmax, grank, gm1 = sb("gmax", [P, NT, NG]), sb("grank", [P, NT, NG]), sb("gm1", [P, NT, NG])
        qp = hl[:, 0:2, :]
        ah, al = hl[:, 2, :], hl[:, 3, :]
        ch, cl = hh[:, 0:2, :], hh[:, 2:4, :]
        prob = [hf[:, 0, :], hf[:, 1, :], wy[:, 0, :], wy[:, 1, :]]
        vals = sb("vals", [P, 2, NT, NH, HD + 1])
        sign = sb("sign", [P, 2])
        bvb, bo = sb("bvb", [P, P]), sb("bo", [P, 1])
        maskq, maskk = sb("maskq", [P, HG, P], BF16), sb("maskk", [P, HG, P], BF16)
        ident16 = sb("ident16", [P, P], BF16)
        selm = sb("selm", [2 * HG, HG, P], BF16)
        negmax = sb("negmax", [P, NT, HG])
        nm16 = sb("nm16", [P, NT, HG], BF16)
        nmb = sb("nmb", [P, NT, 2 * HG])
        nmT = sb("nmT", [2 * HG, 2, BT], BF16)
        rden = sb("rden", [P, NT, NH])
        gamma, beta = sb("gamma", [P, 1]), sb("beta", [P, 1])
        b1d, b2d = sb("b1d", [P, CD]), sb("b2d", [P, 1])
        msk = sb("msk", [P, NT, EB])
        rnk = sb("rnk", [P, NT, EB])
        wb = sb("wb", [P, NT, EB])
        wbh = sb("wbh", [P, NT, EB], F32R)
        combA_flat = combA[:].rearrange("p t e -> p (t e)")
        comb = sb("comb", [P, NT * 2 * EB])

        in_x0, in_x, in_small = sem("in_x0"), sem("in_x"), sem("in_small")
        in_raw = [sem(f"in_raw{k}") for k in range(4)]
        in_ctx = [sem(f"in_ctx{k}") for k in range(2)]
        consts, const_step = sem("consts"), sem("const_step")
        raw_hi, raw_lo = sem("raw_hi"), sem("raw_lo")
        logits_done, logits_read = sem("logits_done"), sem("logits_read")
        exp_in, exp_done, routed = sem("exp_in"), sem("exp_done"), sem("routed")
        selr = sem("selr")
        var_ready, rstd_ready, xn_ready = sem("var_ready"), sem("rstd_ready"), sem("xn_ready")
        xT_done, xTh_ready, xTl_ready = sem("xT_done"), sem("xTh_ready"), sem("xTl_ready")
        acc_ready, back_done, x_updated = sem("acc_ready"), sem("back_done"), sem("x_updated")
        dve = sem("dve")
        comb_ready = sem("comb_ready")
        combT_done, combT_ready = sem("combT_done"), sem("combT_ready")
        a_up, a_hf, a_hh, a_hl, a_down = sem("a_up"), sem("a_hf"), sem("a_hh"), sem("a_hl"), sem("a_down")
        a_cb, a_cbs, a_wy, a_acc = sem("a_cb"), sem("a_cbs"), sem("a_wy"), sem("a_acc")
        stored = sem("stored")
        b_up1, b_up3, b_sg, b_hf, b_hh, b_hl = (sem(n) for n in ("b_up1", "b_up3", "b_sg", "b_hf", "b_hh", "b_hl"))
        b_down, b_cb, b_cbs, b_wy, b_acc = (sem(n) for n in ("b_down", "b_cb", "b_cbs", "b_wy", "b_acc"))
        c_proj, c_r, c_qk, c_kd, c_qd = (sem(n) for n in ("c_proj", "c_r", "c_qk", "c_kd", "c_qd"))
        c_s1, c_max, c_nm, c_nmt, c_nmT = (sem(n) for n in ("c_s1", "c_max", "c_nm", "c_nmt", "c_nmT"))
        c_s2, c_exp, c_pv, c_vp, c_v = (sem(n) for n in ("c_s2", "c_exp", "c_pv", "c_vp", "c_v"))
        c_ch, c_cl, c_norm, c_ot, c_ah, c_al, c_wo = (sem(n) for n in ("c_ch", "c_cl", "c_norm", "c_ot", "c_ah", "c_al", "c_wo"))
        c_ctx = [sem(f"c_ctx{k}") for k in range(2)]
        in_scales, dequant, beta_done, diag_clear = sem("in_scales"), sem("dequant"), sem("beta_done"), sem("diag_clear")
        d_up, d_hf, d_hh, d_hl, d_down = (sem(n) for n in ("d_up", "d_hf", "d_hh", "d_hl", "d_down"))
        b_logits, b_sgm, wgb_split = sem("b_logits"), sem("b_sgm"), sem("wgb_split")
        bcomb_ready, bcombT_done, bcombT_ready = sem("bcomb_ready"), sem("bcombT_done"), sem("bcombT_ready")

        def blk(i, p, shift):
            return (i * 2 + (p + shift + NB)) % NB

        def at(stage, i, p, per_block, count):
            return i * (2 * per_block) + ((stage * NB + p) * per_block + count)

        def mm3(dst, wh, wl, xh, xl, start=True, stop=True):
            nc.tensor.matmul(dst, wh, xh, start=start, stop=False)
            nc.tensor.matmul(dst, wh, xl, start=False, stop=False)
            return nc.tensor.matmul(dst, wl, xh, start=False, stop=stop)

        class Chain:
            def __init__(self, eng):
                self.eng, self.base, self.n = eng, 0, 0

            def begin(self, i, p, per_block, start):
                self.per, self.n = per_block, 0
                self.base = i * (2 * per_block) + (start + p * per_block)

            def __call__(self, ins):
                ins.then_inc(dve, 1)
                self.n += 1
                self.eng.wait_ge(dve, self.base + self.n)

            def end(self):
                assert self.n == self.per, (self.n, self.per)

        HID, HF, HH, YB, CBB = 4, 2, 4, 2, 1

        NS = 4
        block = ctx.enter_context(nc.Block())

        def flat(v):
            return v if len(v.shape) == 2 else v.rearrange(
                "p a b -> p (a b)" if len(v.shape) == 3 else "p a b c -> p (a b c)")

        raw_src = []
        for e in range(EA):
            raw_src.append((a_w1[:, e * FA:(e + 1) * FA], w1h[:, e, :], w1l[:, e, :]))
            raw_src.append((a_w2[:, e * FA:(e + 1) * FA], flat(w2h[:, e]), flat(w2l[:, e])))
        EQ = BT // P
        for src, wh, wl in ((b_w1, bw1h, bw1l), (b_w3, bw3h, bw3l)):
            for q in range(EB // EQ):
                raw_src.append((src[:, q * BT:(q + 1) * BT], flat(wh[:, q * EQ:(q + 1) * EQ]), flat(wl[:, q * EQ:(q + 1) * EQ])))
        NRAW0 = len(raw_src)
        for q in range(EB // EQ):
            raw_src.append((b_w2[:, q * BT:(q + 1) * BT], flat(bw2h[:, q * EQ:(q + 1) * EQ]), flat(bw2l[:, q * EQ:(q + 1) * EQ])))
        NRAW1 = len(raw_src)
        for q in range(2):
            raw_src.append((c_wqk[:, q * BT:(q + 1) * BT], flat(wqkh[:, q]), flat(wqkl[:, q])))
        raw_src.append((c_wvo, flat(wvoh), flat(wvol)))
        NRAW2 = len(raw_src)
        raw_src.append((d_fc1, fc1h, fc1l))
        raw_src.append((d_fc2, flat(fc2h), flat(fc2l)))
        NRAW = len(raw_src)

        SMALL = ((wga, a_wg), (bga, a_bg), (b1a, a_b1), (b2a, a_b2), (wgb, b_wg), (b1b, b_b1), (b3b, b_b3), (b2b, b_b2),
                 (sign, c_sign), (bvb, c_bv), (bo, c_bo), (gamma, d_gamma), (beta, d_beta), (b1d, d_b1), (b2d, d_b2))

        @block.sync
        def _(sp):
            for dst, src in SMALL:
                sp.dma_start(dst[:], src).then_inc(in_small, 16)
            for k in range(4):
                sp.dma_start(raw[:, k, :], raw_src[k][0]).then_inc(in_raw[k], 16)
            for b in range(NB):
                if b >= 2:
                    sp.wait_ge(logits_done, b - 1)
                sp.dma_start(ctxr[:, b % 2, :], ctxT[:, b * BT:(b + 1) * BT]).then_inc(in_ctx[b % 2], 16)
                if b == 0:
                    sp.dma_start(X[:, 0:BT].rearrange("p (t d) -> p t d", t=NT),
                                 x[0:BT, :].rearrange("(t p) d -> p t d", p=P)).then_inc(in_x0, 16)
            for b in range(1, NB):
                sp.dma_start(X[:, b * BT:(b + 1) * BT].rearrange("p (t d) -> p t d", t=NT),
                             x[b * BT:(b + 1) * BT, :].rearrange("(t p) d -> p t d", p=P)).then_inc(in_x, 16)
            for k in range(4, NRAW):
                if k == NRAW - 1:
                    sp.wait_ge(b_hl, NB * EB + HF)
                    sp.dma_start(sg[:], d_scales.rearrange("p (k n) -> p k n", k=2)).then_inc(in_scales, 16)
                sp.wait_ge(raw_lo, k - 3)
                src = raw_src[k][0]
                dst = raw[:, k % 4, 0:src.shape[1]]
                sp.dma_start(dst if k < NRAW2 else dst.bitcast(I32), src).then_inc(in_raw[k % 4], 16)
            sp.dma_start(ctxr[:, 0, :], ctxT[:, 0:BT]).then_inc(c_ctx[0], 16)
            with sp.Fori(0, NB // 2) as i:
                for p in range(2):
                    sp.wait_ge(c_cl, at(0, i, p, 1, 1))
                    sp.dma_start(ctxr[:, 1 - p, :], ctxT[:, bass.ds(blk(i, p, 1) * BT, BT)]).then_inc(c_ctx[1 - p], 16)
            for b in range(NB):
                sp.wait_ge(x_updated, STAGE_D * NB + 2 + b)
                sp.dma_start(out[b * BT:(b + 1) * BT, :].rearrange("(t p) d -> p t d", p=P),
                             X[:, b * BT:(b + 1) * BT].rearrange("p (t d) -> p t d", t=NT)).then_inc(stored, 16)
            sp.wait_ge(stored, 16 * NB)

        @block.gpsimd
        def _(pool):
            g = nc.gpsimd
            n = 0

            def step(ins):
                nonlocal n
                ins.then_inc(const_step, 1)
                n += 1
                pool.wait_ge(const_step, n)
            g.memset(mhalf[:], -0.5)
            g.memset(accT[:, 1, :], 0.0).then_inc(acc_ready, 1)
            step(g.memset(ident[:], 0.0))
            step(g.affine_select(out=ident[:], in_=ident[:], compare_op=ALU.not_equal, fill=1.0, base=0,
                                 pattern=[[-1, P]], channel_multiplier=1))
            step(g.memset(lower[:], 1.0))
            step(g.memset(upper[:], 1.0))
            step(g.affine_select(out=lower[:], in_=lower[:], compare_op=ALU.is_gt, fill=0.0, base=0,
                                 pattern=[[1, EB], [-1, EB]], channel_multiplier=0))
            step(g.affine_select(out=upper[:], in_=upper[:], compare_op=ALU.is_ge, fill=0.0, base=0,
                                 pattern=[[-1, EB], [1, EB]], channel_multiplier=0))
            step(g.memset(maskq[:], 0.0))
            step(g.memset(maskk[:], 0.0))
            step(g.affine_select(out=maskq[:], in_=maskq[:], compare_op=ALU.is_gt, fill=MASKED, base=0,
                                 pattern=[[0, HG], [-1, P]], channel_multiplier=1))
            step(g.affine_select(out=maskk[:], in_=maskk[:], compare_op=ALU.is_gt, fill=MASKED, base=0,
                                 pattern=[[0, HG], [1, P]], channel_multiplier=-1))
            g.memset(maskq[0:1, :, 0:1], 0.0)
            g.memset(maskk[0:1, :, 0:1], 0.0)
            g.memset(vals[:], 1.0)
            g.memset(veps[:], 1.0).then_inc(consts, 1)

            def rstd_step(stage, i, p):
                pool.wait_ge(var_ready, at(stage, i, p, 1, 2))
                g.tensor_tensor(rstd[:], veps[:], mhalf[:], ALU.pow).then_inc(rstd_ready, 1)

            pool.wait_ge(var_ready, 1)
            g.tensor_tensor(rstd[:], veps[:], mhalf[:], ALU.pow).then_inc(rstd_ready, 1)

            def sum_experts(i, p, stage, E, wy_ready, acc):
                rstd_step(stage, i, p)
                for e in range(1, E):
                    pool.wait_ge(wy_ready, at(0, i, p, E, e + 1 + YB))
                    if e > 1:
                        pool.wait_ge(acc, at(0, i, p, E - 2, e - 1))
                    g.tensor_tensor(accT[:, p, :], accT[:, p, :], wy[:, e % 2, :],
                                    ALU.add).then_inc(acc if e < E - 1 else acc_ready, 1)

            with pool.Fori(0, NB // 2) as i:
                for p in range(2):
                    sum_experts(i, p, STAGE_A, EA, a_wy, a_acc)
            pool.wait_ge(a_down, NB * UA + HH)
            g.memset(region1[:, 0:4 * NT * BT].bitcast(F32), 0.0).then_inc(diag_clear, 1)
            with pool.Fori(0, NB // 2) as i:
                for p in range(2):
                    sum_experts(i, p, STAGE_B, EB, b_wy, b_acc)
            for stage in (STAGE_C, STAGE_D):
                with pool.Fori(0, NB // 2) as i:
                    for p in range(2):
                        rstd_step(stage, i, p)

        def ln_stats(eng, link, off, first=None):
            for t in range(NT):
                ins = nc.vector.bn_stats(st[:, t, :], X[:, bass.ds(off + t * P, P)])
            link(ins)
            nc.vector.memset(carry[:], 0.0)
            for t in range(NT):
                ins = nc.vector.bn_aggr(mv[:, t, :], st[:, t, :])
            link(ins)
            nc.vector.tensor_scalar_add(veps[:], mv[:, :, 1], EPS).then_inc(var_ready, 1)

        def ln_apply(off):
            for t in range(NT):
                ins = nc.vector.tensor_scalar(xn[:, t * P:(t + 1) * P], X[:, bass.ds(off + t * P, P)],
                                              mv[:, t, 0:1], rstd[:, t:t + 1], ALU.subtract, ALU.mult)
            ins.then_inc(xn_ready, 1)

        def spread(v, *dims):
            return bass.AP(v.tensor, v.offset, [list(v.ap[0])] + [list(d) for d in dims])

        def rank_of(link, vals, T, E, dst):
            own = spread(vals, [E, T], [1, E], [0, E])
            other = spread(vals, [E, T], [0, E], [1, E])
            low, upp = (spread(m[:], [0, T], [EB, E], [1, E]) for m in (lower, upper))
            r1, r2 = (m[:, 0:T * E * E].rearrange("p (t e j) -> p t e j", t=T, e=E) for m in (rk1, rk2))
            v = nc.vector
            v.tensor_tensor(r1, other, own, ALU.is_ge)
            link(v.tensor_tensor(r2, other, own, ALU.is_gt))
            v.tensor_tensor(r1, r1, low, ALU.mult)
            link(v.tensor_tensor(r2, r2, upp, ALU.mult))
            link(v.tensor_tensor(r1, r1, r2, ALU.add))
            link(v.tensor_reduce(dst, r1, AX, ALU.add))
        RANK_LINKS = 4

        def write_back(eng, stage, i, p):
            eng.wait_ge(back_done, at(stage, i, p, 1, 1))
            xs = X[:, bass.ds(blk(i, p, -1) * BT, BT)]
            nc.vector.tensor_tensor(xs, xs, tr_ps[:], ALU.add).then_inc(x_updated, 1)
            eng.wait_ge(x_updated, at(stage, i, p, 1, 1))

        def apply_next(eng, stage, i, p):
            eng.wait_ge(rstd_ready, at(stage, i, p, 1, 2))
            ln_apply(blk(i, p, 1) * BT)

        def low_next(eng, stage, i, p):
            eng.wait_ge(xTh_ready, at(stage, i, p, 1, 2))
            nc.vector.tensor_tensor(xTl[:, 1 - p, :], tr_ps[:], xTh[:, 1 - p, :].bitcast(F32),
                                    ALU.subtract).then_inc(xTl_ready, 1)

        def high_next(eng, stage, i, p):
            eng.wait_ge(xT_done, at(stage, i, p, 1, 2))
            nc.scalar.activation(xTh[:, 1 - p, :], tr_ps[:], ACT.Copy).then_inc(xTh_ready, 1)

        K_DVE_A = 2 + 0

        @block.vector
        def _(eng):
            v = nc.vector
            link = Chain(eng)
            PRO = 2 + 100
            link.per, link.n, link.base = 10 ** 6, 0, 0
            eng.sem_inc(a_hl, HF)
            eng.sem_inc(a_wy, YB)
            eng.sem_inc(b_hf, 2)
            eng.sem_inc(c_max, 2)
            eng.sem_inc(c_norm, 1)
            eng.sem_inc(c_al, 1)
            eng.sem_inc(d_hl, 2)
            eng.sem_inc(b_hl, HF)
            eng.sem_inc(b_wy, YB)
            eng.wait_ge(consts, 1)
            eng.wait_ge(in_x0, 16)
            ln_stats(eng, link, 0)
            def split_low(k):
                eng.wait_ge(raw_hi, k + 1)
                src, wh, wl = raw_src[k]
                v.tensor_tensor(wl, raw[:, k % 4, 0:src.shape[1]], wh.bitcast(F32), ALU.subtract).then_inc(raw_lo, 1)

            def selector(E):
                return v.tensor_tensor(sel[0:2 * E, 0:E, :], spread(ident[0:2 * E, 0:E], [1, E], [0, P]),
                                       spread(ident[0:2 * E, E:2 * E], [1, E], [0, P]), ALU.add)
            for k in range(NRAW0):
                split_low(k)
                if k == 1:
                    eng.wait_ge(rstd_ready, 1)
                    ln_apply(0)
                if k == 5:
                    eng.wait_ge(xTh_ready, 1)
                    v.tensor_tensor(xTl[:, 0, :], tr_ps[:], xTh[:, 0, :].bitcast(F32), ALU.subtract).then_inc(xTl_ready, 1)
            selector(EA).then_inc(selr, 1)
            eng.wait_ge(logits_done, NB)
            eng.wait_ge(in_small, 16 * len(SMALL))
            lgp = cb_ps[:, 0:TA * EA].rearrange("p (t e) -> p t e", e=EA)
            link(v.tensor_tensor(lga[:], lgp, spread(bga[:], [0, TA], [1, EA]), ALU.add))
            for t0 in range(0, TA, TH):
                rank_of(link, lga[:, t0:t0 + TH, :], TH, EA, rank[:, t0:t0 + TH, :])
            link(v.tensor_reduce(mx[:], lga[:], AX, ALU.max))
            v.tensor_tensor(ex[:], lga[:], spread(mx[:], [1, TA], [0, EA]), ALU.subtract).then_inc(exp_in, 1)
            link(v.tensor_scalar(rank[:], rank[:], 1.5, None, ALU.is_lt))
            eng.wait_ge(exp_done, 1)
            link(v.tensor_tensor(ex[:], ex[:], rank[:], ALU.mult))
            link(v.tensor_reduce(ssum[:], ex[:], AX, ALU.add))
            link(v.reciprocal(ssum[:], ssum[:]))
            link(v.tensor_tensor(ex[:], ex[:], spread(ssum[:], [1, TA], [0, EA]), ALU.mult))
            link(v.tensor_copy(hi32[:], ex[:]))
            v.tensor_copy(combA[:, :, 0:EA], hi32[:].bitcast(F32))
            v.tensor_tensor(combA[:, :, EA:2 * EA], ex[:], hi32[:].bitcast(F32), ALU.subtract).then_inc(routed, 1)
            eng.wait_ge(in_x, 16 * (NB - 1))
            start = link.n

            with eng.Fori(0, NB // 2) as i:
                for p in range(2):
                    link.begin(i, p, 2, start)

                    def weigh(e):
                        eng.wait_ge(a_down, at(0, i, p, UA, (e + 1) * CA + HH))
                        eng.wait_ge(a_cbs, at(0, i, p, EA, e + 1 + CBB))
                        if e >= 3:
                            eng.wait_ge(a_acc, at(0, i, p, EA - 2, e - 2))
                        elif e:
                            eng.wait_ge(acc_ready, at(STAGE_A, i, p, 1, 1))
                        dst = accT[:, p, :] if e == 0 else wy[:, e % 2, :]
                        v.scalar_tensor_tensor(dst, y_ps[e % 2][:], b2a[:, e:e + 1], cbs[:, e % 2, :],
                                               op0=ALU.add, op1=ALU.mult).then_inc(a_wy, 1)
                    for u in range(UA):
                        eng.wait_ge(a_hf, at(0, i, p, UA, u + 1 + HID))
                        eng.wait_ge(a_down, at(0, i, p, UA, u + 1))
                        v.tensor_copy(hh[:, u % 4, :], hf[:, u % 2, :]).then_inc(a_hh, 1)
                        eng.wait_ge(a_hh, at(0, i, p, UA, u + 1))
                        v.tensor_tensor(hl[:, u % 4, :], hf[:, u % 2, :], hh[:, u % 4, :].bitcast(F32),
                                        ALU.subtract).then_inc(a_hl, 1)
                        if u == 5:
                            write_back(eng, STAGE_A, i, p)
                        if u == 8:
                            ln_stats(eng, link, blk(i, p, 1) * BT)
                        if u == 13:
                            apply_next(eng, STAGE_A, i, p)
                        if u == 19:
                            low_next(eng, STAGE_A, i, p)
                        if u % CA == CA - 1 and u > CA:
                            weigh(u // CA - 1)
                    weigh(EA - 1)
                    link.end()
            start += NB * 2

            for k in range(NRAW0, NRAW1):
                split_low(k)
            link.per, link.n, link.base = 10 ** 6, 0, start
            link(v.tensor_copy(wgbh[:], wgb[:]))
            v.tensor_tensor(wgbl[:], wgb[:], wgbh[:].bitcast(F32), ALU.subtract).then_inc(wgb_split, 1)
            selector(EB).then_inc(selr, 1)

            def choose_groups(link):
                link(v.tensor_reduce(gmax[:], spread(sgm[:], [EB // NG, NT * NG], [1, EB // NG]), AX, ALU.max))
                rank_of(link, gmax[:], NT, NG, grank[:])
                link(v.tensor_scalar(grank[:], grank[:], 1.5, None, ALU.is_lt))
                v.tensor_scalar_add(gm1[:], grank[:], -1.0)
                each = [1, NT * NG], [0, EB // NG]
                m = spread(msk[:], [EB // NG, NT * NG], [1, EB // NG])
                link(v.tensor_tensor(m, spread(sgm[:], [EB // NG, NT * NG], [1, EB // NG]), spread(grank[:], *each), ALU.mult))
                link(v.tensor_tensor(m, m, spread(gm1[:], *each), ALU.add))

            def choose_experts(link):
                rank_of(link, msk[:], NT, EB, rnk[:])

            def route_weights(link):
                link(v.tensor_scalar(rnk[:], rnk[:], 3.5, None, ALU.is_lt))
                link(v.tensor_tensor(wb[:], sgm[:], rnk[:], ALU.mult))
                link(v.tensor_reduce(ssum[:, 0:NT], wb[:], AX, ALU.add))
                link(v.reciprocal(ssum[:, 0:NT], ssum[:, 0:NT]))
                link(v.tensor_tensor(wb[:], wb[:], spread(ssum[:], [1, NT], [0, EB]), ALU.mult))
                link(v.tensor_scalar(wb[:], wb[:], ROUTE_SCALE, None, ALU.mult))
                link(v.tensor_copy(wbh[:], wb[:]))
                rows = comb[:].rearrange("p (t s e) -> p t s e", t=NT, s=2)
                v.tensor_copy(rows[:, :, 0, :], wbh[:].bitcast(F32))
                v.tensor_tensor(rows[:, :, 1, :], wb[:], wbh[:].bitcast(F32), ALU.subtract).then_inc(bcomb_ready, 1)
            eng.wait_ge(b_sgm, 1)
            choose_groups(link)
            choose_experts(link)
            route_weights(link)
            start += link.n

            with eng.Fori(0, NB // 2) as i:
                for p in range(2):
                    link.begin(i, p, 2 + 4 + 2 * RANK_LINKS + 7, start)

                    def weigh(e):
                        eng.wait_ge(b_down, at(0, i, p, EB, e + 1 + HH))
                        eng.wait_ge(b_cbs, at(0, i, p, EB, e + 1 + CBB))
                        if e >= 3:
                            eng.wait_ge(b_acc, at(0, i, p, EB - 2, e - 2))
                        elif e:
                            eng.wait_ge(acc_ready, at(STAGE_B, i, p, 1, 1))
                        dst = accT[:, p, :] if e == 0 else wy[:, e % 2, :]
                        v.scalar_tensor_tensor(dst, y_ps[e % 2][:], b2b[:, e:e + 1], cbs[:, e % 2, :],
                                               op0=ALU.add, op1=ALU.mult).then_inc(b_wy, 1)

                    def low(e):
                        eng.wait_ge(b_hh, at(0, i, p, EB, e + 1))
                        eng.wait_ge(b_down, at(0, i, p, EB, e + 1))
                        v.tensor_tensor(hl[:, e % 4, :], hf[:, e % 2, :], hh[:, e % 4, :].bitcast(F32),
                                        ALU.subtract).then_inc(b_hl, 1)
                    for e in range(EB):
                        eng.wait_ge(b_sg, at(0, i, p, EB, e + 1 + 2))
                        eng.wait_ge(b_up3, at(0, i, p, EB, e + 1))
                        eng.wait_ge(b_hl, at(0, i, p, EB, e + 1))
                        v.scalar_tensor_tensor(hf[:, e % 2, :], hid_ps[2 + e % 2][:], b3b[:, e:e + 1], sg[:, e % 2, :],
                                               op0=ALU.add, op1=ALU.mult).then_inc(b_hf, 1)
                        if e >= 1:
                            low(e - 1)
                        if e >= 3:
                            weigh(e - 3)
                        if e == 2:
                            write_back(eng, STAGE_B, i, p)
                        if e == 3:
                            ln_stats(eng, link, blk(i, p, 1) * BT)
                        if e == 5:
                            apply_next(eng, STAGE_B, i, p)
                        if e == 8:
                            low_next(eng, STAGE_B, i, p)
                        if e == 11:
                            eng.wait_ge(b_sgm, at(0, i, p, 1, 2))
                            choose_groups(link)
                        if e == 12:
                            choose_experts(link)
                        if e == 13:
                            eng.wait_ge(bcombT_done, at(0, i, p, 1, 1))
                            route_weights(link)
                    low(EB - 1)
                    for e in range(EB - 3, EB):
                        weigh(e)
                    link.end()
            start += NB * link.per

            link.per, link.n, link.base = 10 ** 6, 0, start
            for k in range(NRAW1, NRAW2):
                split_low(k)
            eng.wait_ge(in_scales, 16)
            for k in (NRAW2, NRAW2 + 1):
                eng.wait_ge(in_raw[k % 4], 16 * (k // 4 + 1))
                slot = raw[:, k % 4, :]
                v.scalar_tensor_tensor(slot, slot.bitcast(I32), -128.0, sg[:, k - NRAW2, :],
                                       op0=ALU.add, op1=ALU.mult).then_inc(dequant, 1)
            eng.wait_ge(beta_done, 1)
            slot = raw[:, NRAW2 % 4, :]
            v.tensor_scalar(slot, slot, gamma[:, 0:1], None, ALU.mult).then_inc(dequant, 1)
            v.tensor_tensor(b1d[:], b1d[:], cb_ps[:, 0:CD], ALU.add).then_inc(dequant, 1)
            for k in range(NRAW2, NRAW):
                split_low(k)
            v.tensor_copy(ident16[:], ident[:])
            v.tensor_tensor(selm[:], spread(ident[0:2 * HG, 0:HG], [1, HG], [0, P]),
                            spread(ident[0:2 * HG, HG:2 * HG], [1, HG], [0, P]), ALU.add).then_inc(selr, 1)

            def at4(i, p, g, ahead, per_step, count):
                return i * (2 * SG * per_step) + ((p * SG + g + ahead) * per_step + count)

            def max_of(i, p, g, b):
                eng.wait_ge(c_s1, at4(i, p, g, 1, NT, b + 1))
                v.tensor_reduce(negmax[:, b, :], hid_ps[b % 2][:].rearrange("p (i k) -> p i k", i=HG), AX, ALU.max,
                                negate=True).then_inc(c_max, 1)

            def split_max(i, p, g):
                eng.wait_ge(c_max, at4(i, p, g, 1, NT, NT + 2))
                link(v.tensor_copy(nm16[:], negmax[:]))
                v.tensor_copy(nmb[:, :, 0:HG], nm16[:])
                v.tensor_tensor(nmb[:, :, HG:], negmax[:], nm16[:], ALU.subtract).then_inc(c_nm, 1)

            def pack(i, p, g, which):
                eng.wait_ge(c_r, at4(i, p, g, 2, 2, which + 1))
                dst = kp[:, (g + 2) % 4, :] if which else qp[:, g % 2, :]
                v.scalar_tensor_tensor(dst, cbs[:, which, :], sign[:, which:which + 1], cb_ps[:],
                                       op0=ALU.mult, op1=ALU.add).then_inc(c_qk, 1)

            def spread_q(i, p, g):
                eng.wait_ge(c_qk, at4(i, p, g, 2, 2, 1))
                for h in range(HG):
                    rows = slice(32 * h, 32 * h + 32)
                    ins = v.tensor_copy(qdiag[g % 2][rows, :, h * P:(h + 1) * P],
                                        qp[rows, g % 2, :].rearrange("p (b k) -> p b k", b=NT))
                ins.then_inc(c_qd, 1)

            def values(par, n):
                eng.wait_ge(c_vp, n)
                v.tensor_tensor(vals[:, par, :, :, 0:HD].rearrange("p b h d -> p (b h) d"),
                                cb_ps[:].rearrange("p (b d) -> p b d", d=HD),
                                spread(bvb[:], [0, NT], [HD, NH], [1, HD]), ALU.add).then_inc(c_v, 1)

            def ctx_low(par, n):
                eng.wait_ge(c_ch, n)
                v.tensor_tensor(cl[:, par, :], ctxr[:, par, :], ch[:, par, :].bitcast(F32), ALU.subtract).then_inc(c_cl, 1)
            ctx_low(0, 1)
            eng.wait_ge(diag_clear, 1)
            for g in (-2, -1):
                pack(0, 0, g, 0)
                pack(0, 0, g, 1)
                spread_q(0, 0, g)
            values(0, 1)
            for b in range(NT):
                max_of(0, 0, -1, b)
            split_max(0, 0, -1)
            start += link.n

            with eng.Fori(0, NB // 2) as i:
                for p in range(2):
                    link.begin(i, p, 2 + SG + 1, start)
                    for g in range(SG):
                        for b in range(NT):
                            max_of(i, p, g, b)
                            if g == 0 and b == 2:
                                write_back(eng, STAGE_C, i, p)
                                ctx_low(1 - p, at(0, i, p, 1, 2))
                            if g == 1 and b == 0:
                                apply_next(eng, STAGE_C, i, p)
                            if g == 1 and b == 3:
                                low_next(eng, STAGE_C, i, p)
                            if b == 2:
                                pack(i, p, g, 0)
                        if g == SG - 1:
                            eng.wait_ge(c_pv, at(0, i, p, SG * NT, SG * NT + 4))
                            for k in range(2):
                                o = y_ps[k][:].rearrange("p (b n) -> p b n", b=2)[:, :, 0:NH * (HD + 1)]
                                ins = v.reciprocal(rden[:, 2 * k:2 * k + 2, :], o.rearrange("p b (h d) -> p b h d", h=NH)[:, :, :, HD])
                            link(ins)
                            for k in range(2):
                                for b in range(2):
                                    o = y_ps[k][:, b * 256:b * 256 + NH * (HD + 1)].rearrange("p (h d) -> p h d", h=NH)[:, :, 0:HD]
                                    bb = 2 * k + b
                                    ins = v.tensor_tensor(xn[:, bb * P:(bb + 1) * P].rearrange("p (h d) -> p h d", h=NH),
                                                          o, spread(rden[:, bb, :], [1, NH], [0, HD]), ALU.mult)
                            ins.then_inc(c_norm, 1)
                        eng.wait_ge(c_nmt, at4(i, p, g, 0, 1, 1))
                        split_max(i, p, g)
                        pack(i, p, g, 1)
                        if g == SG - 1:
                            eng.wait_ge(c_ah, at(0, i, p, 1, 1))
                            v.tensor_tensor(al, tr_ps[:], ah.bitcast(F32), ALU.subtract).then_inc(c_al, 1)
                        eng.wait_ge(c_s2, at4(i, p, g, 0, NT, NT))
                        spread_q(i, p, g)
                        if g == 0:
                            ln_stats(eng, link, blk(i, p, 1) * BT)
                        if g == 2:
                            values(1 - p, at(0, i, p, 1, 2))
                    link.end()
            start += NB * link.per

            with eng.Fori(0, NB // 2) as i:
                for p in range(2):
                    link.begin(i, p, 2, start)

                    def low(c):
                        eng.wait_ge(d_hh, at(0, i, p, CD, c + 1))
                        v.tensor_tensor(hl[:, c, :], hf[:, c % 2, :], hh[:, c, :].bitcast(F32), ALU.subtract).then_inc(d_hl, 1)
                    low(0)
                    write_back(eng, STAGE_D, i, p)
                    low(1)
                    ln_stats(eng, link, blk(i, p, 1) * BT)
                    low(2)
                    apply_next(eng, STAGE_D, i, p)
                    low(3)
                    low_next(eng, STAGE_D, i, p)
                    eng.wait_ge(d_down, at(0, i, p, CD, CD + 4))
                    v.tensor_scalar(accT[:, p, :], y_ps[p][:], b2d[:, 0:1], 0.5, ALU.add, ALU.mult).then_inc(acc_ready, 1)
                    link.end()
            eng.wait_ge(back_done, NB * NS + 1)
            xs = X[:, (NB - 1) * BT:]
            v.tensor_tensor(xs, xs, tr_ps[:], ALU.add).then_inc(x_updated, 1)

        @block.scalar
        def _(eng):
            a = nc.scalar
            eng.sem_inc(a_hf, HID)
            eng.sem_inc(a_cbs, CBB)
            eng.sem_inc(b_sg, 2)
            eng.sem_inc(b_cbs, CBB)

            eng.sem_inc(c_exp, 2)
            eng.sem_inc(d_hf, 4)

            def split_high(k):
                eng.wait_ge(in_raw[k % 4], 16 * (k // 4 + 1))
                src, wh, _ = raw_src[k]
                a.activation(wh, raw[:, k % 4, 0:src.shape[1]], ACT.Copy).then_inc(raw_hi, 1)
            for k in range(NRAW0):
                split_high(k)
                if k == 4:
                    eng.wait_ge(xT_done, 1)
                    a.activation(xTh[:, 0, :], tr_ps[:], ACT.Copy).then_inc(xTh_ready, 1)
            eng.wait_ge(exp_in, 1)
            a.activation(ex[:], ex[:], ACT.Exp).then_inc(exp_done, 1)
            eng.wait_ge(routed, 1)
            a.activation(comb[:, 0:NT * 2 * EA], combA_flat[:, 0:NT * 2 * EA], ACT.Copy).then_inc(comb_ready, 1)
            eng.wait_ge(combT_done, 1)
            a.activation(combT[0:2 * EA, 0, :], tr_ps[0:2 * EA, :], ACT.Copy).then_inc(combT_ready, 1)

            with eng.Fori(0, NB // 2) as i:
                for p in range(2):
                    for u in range(UA):
                        eng.wait_ge(a_up, at(0, i, p, UA, u + 1))
                        eng.wait_ge(a_hl, at(0, i, p, UA, u + 1))
                        a.activation(hf[:, u % 2, :], hid_ps[u % 4][:], ACT.Relu,
                                     bias=b1a[:, u:u + 1]).then_inc(a_hf, 1)
                        if u % CA == 2:
                            e = u // CA
                            eng.wait_ge(a_cb, at(0, i, p, EA, e + 1))
                            eng.wait_ge(a_wy, at(0, i, p, EA, e + 1))
                            a.activation(cbs[:, e % 2, :], cb_ps[:], ACT.Copy).then_inc(a_cbs, 1)
                        if u == 18:
                            high_next(eng, STAGE_A, i, p)
                        if u == 20:
                            eng.wait_ge(combT_ready, at(0, i, p, 1, 1))
                            a.activation(comb[:, 0:NT * 2 * EA],
                                         combA_flat[:, bass.ds(blk(i, p, 1) * (NT * 2 * EA), NT * 2 * EA)],
                                         ACT.Copy).then_inc(comb_ready, 1)
                        if u == 26:
                            eng.wait_ge(combT_done, at(0, i, p, 1, 2))
                            a.activation(combT[0:2 * EA, 1 - p, :], tr_ps[0:2 * EA, :], ACT.Copy).then_inc(combT_ready, 1)

            eng.wait_ge(a_down, NB * UA + HH)
            for k in range(NRAW0, NRAW1):
                split_high(k)

            def scores(n):
                eng.wait_ge(b_logits, n)
                a.activation(sgm[:].rearrange("p t e -> p (t e)"), tr_ps[:, 0:NT * EB], ACT.Sigmoid).then_inc(b_sgm, 1)
            scores(1)
            eng.wait_ge(bcombT_done, 1)
            a.activation(combT[:, 0, :], tr_ps[0:2 * EB, :], ACT.Copy).then_inc(bcombT_ready, 1)
            with eng.Fori(0, NB // 2) as i:
                for p in range(2):
                    def high(e):
                        eng.wait_ge(b_hf, at(0, i, p, EB, e + 1 + 2))
                        eng.wait_ge(b_down, at(0, i, p, EB, e + 1))
                        a.activation(hh[:, e % 4, :], hf[:, e % 2, :], ACT.Copy).then_inc(b_hh, 1)

                    def weight(e):
                        eng.wait_ge(b_cb, at(0, i, p, EB, e + 1))
                        eng.wait_ge(b_wy, at(0, i, p, EB, e + 1))
                        a.activation(cbs[:, e % 2, :], cb_ps[:], ACT.Copy).then_inc(b_cbs, 1)
                    for e in range(EB):
                        eng.wait_ge(b_up1, at(0, i, p, EB, e + 1))
                        eng.wait_ge(b_hf, at(0, i, p, EB, e + 1))
                        a.activation(sg[:, e % 2, :], hid_ps[e % 2][:], ACT.Silu, bias=b1b[:, e:e + 1]).then_inc(b_sg, 1)
                        if e >= 1:
                            high(e - 1)
                        if e >= 2:
                            weight(e - 2)
                        if e == 7:
                            high_next(eng, STAGE_B, i, p)
                        if e == 10:
                            scores(at(0, i, p, 1, 2))
                    high(EB - 1)
                    weight(EB - 2)
                    weight(EB - 1)
                    eng.wait_ge(bcombT_done, at(0, i, p, 1, 2))
                    a.activation(combT[:, 1 - p, :], tr_ps[0:2 * EB, :], ACT.Copy).then_inc(bcombT_ready, 1)

            eng.wait_ge(b_down, NB * EB + HH)
            for k in range(NRAW1, NRAW2):
                split_high(k)
            eng.wait_ge(dequant, 3)
            for k in range(NRAW2, NRAW):
                split_high(k)

            def at4(i, p, g, ahead, per_step, count):
                return i * (2 * SG * per_step) + ((p * SG + g + ahead) * per_step + count)

            def ctx_high(par, arrived):
                eng.wait_ge(c_ctx[par], arrived)
                a.activation(ch[:, par, :], ctxr[:, par, :], ACT.Copy).then_inc(c_ch, 1)

            def rounded(i, p, g, which):
                eng.wait_ge(c_proj, at4(i, p, g, 2, 2, which + 1))
                if not (isinstance(i, int) and g == -2):
                    eng.wait_ge(c_qk, at4(i, p, g, 1, 2, which + 1))
                a.activation(cbs[:, which, :].bitcast(F32R), cb_ps[:], ACT.Copy).then_inc(c_r, 1)

            def spread_k(i, p, g):
                eng.wait_ge(c_qk, at4(i, p, g, 2, 2, 2))
                for h in range(HG):
                    rows = slice(32 * h, 32 * h + 32)
                    ins = a.activation(kdiag[g % 2][rows, :, h * P:(h + 1) * P],
                                       kp[rows, (g + 2) % 4, :].bitcast(F32).rearrange("p (b k) -> p b k", b=NT), ACT.Copy)
                ins.then_inc(c_kd, 1)

            def shifts(i, p, g):
                eng.wait_ge(c_nmt, at4(i, p, g, 1, 1, 1))
                a.activation(nmT[:, (g + 1) % 2, :], tr_ps[0:2 * HG, :], ACT.Copy).then_inc(c_nmT, 1)
            ctx_high(0, 16)
            eng.wait_ge(diag_clear, 1)
            for g in (-2, -1):
                rounded(0, 0, g, 0)
                rounded(0, 0, g, 1)
                spread_k(0, 0, g)
            shifts(0, 0, -1)
            with eng.Fori(0, NB // 2) as i:
                for p in range(2):
                    for g in range(SG):
                        for b in range(NT):
                            eng.wait_ge(c_s2, at4(i, p, g, 0, NT, b + 1))
                            eng.wait_ge(c_pv, at4(i, p, g, 0, NT, b + 1))
                            a.activation(prob[b], hid_ps[2 + b % 2][:], ACT.Exp, scale=float(HD) ** -0.5).then_inc(c_exp, 1)
                            if b == 1:
                                rounded(i, p, g, 0)
                            if g == 0 and b == 1:
                                ctx_high(1 - p, i * 16 + 16 if p == 0 else i * 16 + 32)
                            if g == 1 and b == 2:
                                high_next(eng, STAGE_C, i, p)
                        rounded(i, p, g, 1)
                        shifts(i, p, g)
                        if g == SG - 1:
                            eng.wait_ge(c_ot, at(0, i, p, 1, 1))
                            a.activation(ah, tr_ps[:], ACT.Copy).then_inc(c_ah, 1)
                        spread_k(i, p, g)
                    eng.wait_ge(c_wo, at(0, i, p, 1, 1))
                    a.activation(accT[:, p, :], cb_ps[:], ACT.Identity, bias=bo[:, 0:1]).then_inc(acc_ready, 1)

            with eng.Fori(0, NB // 2) as i:
                for p in range(2):
                    for c in range(CD):
                        eng.wait_ge(d_up, at(0, i, p, CD, c + 1))
                        eng.wait_ge(d_hl, at(0, i, p, CD, c + 1))
                        a.activation(hf[:, c % 2, :], hid_ps[c][:], ACT.Silu, bias=b1d[:, c:c + 1]).then_inc(d_hf, 1)
                        eng.wait_ge(d_hf, at(0, i, p, CD, c + 1 + 4))
                        eng.wait_ge(d_down, at(0, i, p, CD, c + 1))
                        a.activation(hh[:, c, :], hf[:, c % 2, :], ACT.Copy).then_inc(d_hh, 1)
                    high_next(eng, STAGE_D, i, p)

        @block.tensor
        def _(eng):
            t = nc.tensor
            eng.sem_inc(a_down, HH)
            eng.sem_inc(b_down, HH)
            eng.sem_inc(c_pv, 4)
            eng.sem_inc(d_down, 4)

            def fwd():
                for k in range(NT):
                    ins = t.transpose(tr_ps[:, k * P:(k + 1) * P], xn[:, k * P:(k + 1) * P], ident[:])
                ins.then_inc(xT_done, 1)

            def back(p):
                for k in range(NT):
                    ins = t.transpose(tr_ps[:, k * P:(k + 1) * P], accT[:, p, k * P:(k + 1) * P], ident[:])
                ins.then_inc(back_done, 1)
            eng.wait_ge(consts, 1)
            eng.wait_ge(in_small, 16 * len(SMALL))
            for b in range(NB):
                eng.wait_ge(in_ctx[b % 2], 16 * (b // 2 + 1))
                for k in range(NT):
                    c = (b * NT + k) * EA
                    ins = t.matmul(cb_ps[:, c:c + EA], ctxr[:, b % 2, k * P:(k + 1) * P], wga[:],
                                   start=True, stop=True)
                ins.then_inc(logits_done, 1)
                if b == 1:
                    eng.wait_ge(xn_ready, 1)
                    fwd()

            def comb_transpose(width, done):
                for k in range(NT):
                    ins = t.transpose(tr_ps[0:width, k * P:(k + 1) * P], comb[:, k * width:(k + 1) * width], ident[:])
                ins.then_inc(done, 1)
            eng.wait_ge(xTl_ready, 1)
            eng.wait_ge(comb_ready, 1)
            comb_transpose(2 * EA, combT_done)
            eng.wait_ge(selr, 1)

            with eng.Fori(0, NB // 2) as i:
                for p in range(2):
                    def down(u):
                        e, c = divmod(u, CA)
                        if c == 0:
                            eng.wait_ge(a_wy, at(0, i, p, EA, e + 1))
                        eng.wait_ge(a_hl, at(0, i, p, UA, u + 1 + HF))
                        mm3(y_ps[e % 2][:], w2h[:, e, c, :], w2l[:, e, c, :], hh[:, u % 4, :], hl[:, u % 4, :],
                            start=c == 0, stop=c == CA - 1).then_inc(a_down, 1)
                    eng.wait_ge(xTl_ready, at(STAGE_A, i, p, 1, 1))
                    for u in range(UA):
                        e, c = divmod(u, CA)
                        eng.wait_ge(a_hf, at(0, i, p, UA, u + 1))
                        mm3(hid_ps[u % 4][:], w1h[:, e, c * P:(c + 1) * P], w1l[:, e, c * P:(c + 1) * P],
                            xTh[:, p, :], xTl[:, p, :]).then_inc(a_up, 1)
                        if u >= 2:
                            down(u - 2)
                        if c == 0:
                            if e == 0:
                                eng.wait_ge(combT_ready, at(0, i, p, 1, 1))
                            eng.wait_ge(a_cbs, at(0, i, p, EA, e + 1))
                            t.matmul(cb_ps[:], sel[0:2 * EA, e, :], combT[0:2 * EA, p, :], start=True, stop=True).then_inc(a_cb, 1)
                        if u == 4:
                            eng.wait_ge(acc_ready, at(STAGE_A, i, p, 1, 1))
                            back(1 - p)
                        if u == 17:
                            eng.wait_ge(x_updated, at(STAGE_A, i, p, 1, 1))
                            eng.wait_ge(xn_ready, at(STAGE_A, i, p, 1, 2))
                            fwd()
                        if u == 25:
                            eng.wait_ge(xTl_ready, at(STAGE_A, i, p, 1, 2))
                            eng.wait_ge(comb_ready, at(0, i, p, 1, 2))
                            comb_transpose(2 * EA, combT_done)
                    down(UA - 2)
                    down(UA - 1)
            def router(p):
                for k in range(NT):
                    d = tr_ps[:, k * EB:(k + 1) * EB]
                    t.matmul(d, xTh[:, p, k * P:(k + 1) * P], wgbh[:], start=True, stop=False)
                    t.matmul(d, xTh[:, p, k * P:(k + 1) * P], wgbl[:], start=False, stop=False)
                    ins = t.matmul(d, xTl[:, p, k * P:(k + 1) * P], wgbh[:], start=False, stop=True)
                ins.then_inc(b_logits, 1)
            eng.wait_ge(combT_ready, NB + 1)
            eng.wait_ge(wgb_split, 1)
            router(0)
            eng.wait_ge(bcomb_ready, 1)
            comb_transpose(2 * EB, bcombT_done)
            eng.wait_ge(selr, 2)
            eng.wait_ge(raw_lo, NRAW1)
            with eng.Fori(0, NB // 2) as i:
                for p in range(2):
                    def down(e):
                        eng.wait_ge(b_wy, at(0, i, p, EB, e + 1))
                        eng.wait_ge(b_hl, at(0, i, p, EB, e + 1 + HF))
                        mm3(y_ps[e % 2][:], bw2h[:, e, :], bw2l[:, e, :], hh[:, e % 4, :], hl[:, e % 4, :]).then_inc(b_down, 1)
                        eng.wait_ge(b_cbs, at(0, i, p, EB, e + 1))
                        t.matmul(cb_ps[:], sel[:, e, :], combT[:, p, :], start=True, stop=True).then_inc(b_cb, 1)
                    eng.wait_ge(xTl_ready, at(STAGE_B, i, p, 1, 1))
                    eng.wait_ge(bcombT_ready, at(0, i, p, 1, 1))
                    for e in range(EB):
                        eng.wait_ge(b_sg, at(0, i, p, EB, e + 1))
                        mm3(hid_ps[e % 2][:], bw1h[:, e, :], bw1l[:, e, :], xTh[:, p, :], xTl[:, p, :]).then_inc(b_up1, 1)
                        eng.wait_ge(b_hf, at(0, i, p, EB, e + 1))
                        mm3(hid_ps[2 + e % 2][:], bw3h[:, e, :], bw3l[:, e, :], xTh[:, p, :], xTl[:, p, :]).then_inc(b_up3, 1)
                        if e >= 2:
                            down(e - 2)
                        if e == 1:
                            eng.wait_ge(acc_ready, at(STAGE_B, i, p, 1, 1))
                            back(1 - p)
                        if e == 6:
                            eng.wait_ge(x_updated, at(STAGE_B, i, p, 1, 1))
                            eng.wait_ge(xn_ready, at(STAGE_B, i, p, 1, 2))
                            fwd()
                        if e == 9:
                            eng.wait_ge(xTl_ready, at(STAGE_B, i, p, 1, 2))
                            router(1 - p)
                        if e == 15:
                            eng.wait_ge(bcomb_ready, at(0, i, p, 1, 2))
                            comb_transpose(2 * EB, bcombT_done)
                    down(EB - 2)
                    down(EB - 1)

            eng.wait_ge(bcombT_ready, NB + 1)
            eng.wait_ge(dequant, 1)
            eng.wait_ge(b_cbs, NB * EB + CBB)
            for c in range(CD):
                ins = t.matmul(cb_ps[:, c:c + 1], raw[:, NRAW2 % 4, c * P:(c + 1) * P], beta[:], start=True, stop=True)
            ins.then_inc(beta_done, 1)

            def at4(i, p, g, ahead, per_step, count):
                return i * (2 * SG * per_step) + ((p * SG + g + ahead) * per_step + count)

            def project(i, p, g, which, par):
                xh, xl = (ch[:, par, :], cl[:, par, :]) if which else (xTh[:, par, :], xTl[:, par, :])
                mm3(cb_ps[:], wqkh[:, which, (g + 2) % SG, :], wqkl[:, which, (g + 2) % SG, :], xh, xl).then_inc(c_proj, 1)

            def project_values(par):
                for b in range(NT):
                    bs = slice(b * P, (b + 1) * P)
                    ins = mm3(cb_ps[:, bs], ch[:, par, bs], cl[:, par, bs], wvoh[:, 0, :], wvol[:, 0, :])
                ins.then_inc(c_vp, 1)

            def scores(i, p, g, b):
                eng.wait_ge(c_max, at4(i, p, g, 1, NT, b + 1))
                t.matmul(hid_ps[b % 2][:], ident16[:], maskq[:].rearrange("p i k -> p (i k)"), start=True, stop=False)
                t.matmul(hid_ps[b % 2][:], qp[:, (g + 1) % 2, b * P:(b + 1) * P], kdiag[(g + 1) % 2][:, b, :],
                         start=False, stop=True).then_inc(c_s1, 1)

            def shift_rows(i, p, g):
                eng.wait_ge(c_nm, at4(i, p, g, 1, 1, 1))
                for b in range(NT):
                    ins = t.transpose(tr_ps[0:2 * HG, b * P:(b + 1) * P], nmb[:, b, :], ident[:])
                ins.then_inc(c_nmt, 1)

            def scores_T(i, p, g, b):
                eng.wait_ge(c_exp, at4(i, p, g, 0, NT, b + 1))
                s2 = hid_ps[2 + b % 2]
                t.matmul(s2[:], ident16[:], maskk[:].rearrange("p i k -> p (i k)"), start=True, stop=False)
                for h in range(HG):
                    t.matmul(s2[:, h * P:(h + 1) * P], selm[:, h, :], nmT[:, g % 2, b * P:(b + 1) * P], start=False, stop=False)
                t.matmul(s2[:], kp[:, g, b * P:(b + 1) * P], qdiag[g % 2][:, b, :], start=False, stop=True).then_inc(c_s2, 1)

            def weigh_values(i, p, g, b):
                eng.wait_ge(c_exp, at4(i, p, g, 0, NT, b + 1 + 2))
                for h in range(HG):
                    head = g * HG + h
                    c = (b % 2) * 256 + head * (HD + 1)
                    ins = t.matmul(y_ps[b // 2][:, c:c + HD + 1], prob[b][:, h * P:(h + 1) * P], vals[:, p, b, head, :],
                                   start=True, stop=True)
                ins.then_inc(c_pv, 1)
            eng.wait_ge(dequant, 4)
            eng.wait_ge(raw_lo, NRAW)
            eng.wait_ge(xTl_ready, STAGE_C * NB + 1)
            eng.wait_ge(c_cl, 1)
            for g in (-2, -1):
                for which in range(2):
                    if (g, which) != (-2, 0):
                        eng.wait_ge(c_qk, 2 * (g + 2) + which)
                    project(0, 0, g, which, 0)
            eng.wait_ge(c_qk, 4)
            project_values(0)
            eng.wait_ge(selr, 3)
            eng.wait_ge(c_kd, 1)
            eng.wait_ge(acc_ready, STAGE_C * NB + 1)
            for b in range(NT):
                scores(0, 0, -1, b)
            shift_rows(0, 0, -1)
            with eng.Fori(0, NB // 2) as i:
                for p in range(2):
                    for g in range(SG):
                        par = p if g < 2 else 1 - p
                        eng.wait_ge(c_kd, at4(i, p, g, 1, 1, 1))
                        eng.wait_ge(c_qd, at4(i, p, g, 0, 1, 1))
                        eng.wait_ge(c_nmT, at4(i, p, g, 0, 1, 1))
                        if g == 0:
                            eng.wait_ge(c_v, at(0, i, p, 1, 1))
                            eng.wait_ge(c_norm, at(0, i, p, 1, 1))
                        for b in range(NT):
                            scores(i, p, g, b)
                            scores_T(i, p, g, b)
                            if b:
                                weigh_values(i, p, g, b - 1)
                            if g == 0 and b == 1:
                                eng.wait_ge(acc_ready, at(STAGE_C, i, p, 1, 1))
                                eng.wait_ge(c_al, at(0, i, p, 1, 1))
                                back(1 - p)
                            if g == 1 and b == 1:
                                eng.wait_ge(xn_ready, at(STAGE_C, i, p, 1, 2))
                                fwd()
                            if b == 1:
                                eng.wait_ge(c_qk, at4(i, p, g, 2, 2, 0))
                                if g == 2:
                                    eng.wait_ge(xTl_ready, at(STAGE_C, i, p, 1, 2))
                                    eng.wait_ge(c_cl, at(0, i, p, 1, 2))
                                if g == 3:
                                    eng.wait_ge(c_v, at(0, i, p, 1, 2))
                                project(i, p, g, 0, par)
                        weigh_values(i, p, g, NT - 1)
                        eng.wait_ge(c_qk, at4(i, p, g, 2, 2, 1))
                        project(i, p, g, 1, par)
                        if g == 0:
                            eng.wait_ge(x_updated, at(STAGE_C, i, p, 1, 1))
                        if g == 1:
                            eng.wait_ge(xTl_ready, at(STAGE_C, i, p, 1, 2))
                        shift_rows(i, p, g)
                        if g == 2:
                            eng.wait_ge(c_qk, at4(i, p, g, 2, 2, 2))
                            project_values(1 - p)
                    eng.wait_ge(c_nmT, at4(i, p, SG - 1, 1, 1, 1))
                    eng.wait_ge(c_norm, at(0, i, p, 1, 2))
                    for b in range(NT):
                        ins = t.transpose(tr_ps[:, b * P:(b + 1) * P], xn[:, b * P:(b + 1) * P], ident[:])
                    ins.then_inc(c_ot, 1)
                    eng.wait_ge(c_qk, at4(i, p, SG - 1, 2, 2, 2))
                    eng.wait_ge(c_al, at(0, i, p, 1, 2))
                    mm3(cb_ps[:], wvoh[:, 1, :], wvol[:, 1, :], ah, al).then_inc(c_wo, 1)

            with eng.Fori(0, NB // 2) as i:
                for p in range(2):
                    def up(c):
                        eng.wait_ge(d_hf, at(0, i, p, CD, c + 1))
                        mm3(hid_ps[c][:], fc1h[:, c * P:(c + 1) * P], fc1l[:, c * P:(c + 1) * P],
                            xTh[:, p, :], xTl[:, p, :]).then_inc(d_up, 1)

                    def down(c):
                        eng.wait_ge(d_hl, at(0, i, p, CD, c + 1 + 2))
                        mm3(y_ps[p][:], fc2h[:, c, :], fc2l[:, c, :], hh[:, c, :], hl[:, c, :],
                            start=c == 0, stop=c == CD - 1).then_inc(d_down, 1)
                    eng.wait_ge(xTl_ready, at(STAGE_D, i, p, 1, 1))
                    up(0)
                    up(1)
                    eng.wait_ge(acc_ready, at(STAGE_D, i, p, 1, 1))
                    back(1 - p)
                    up(2)
                    down(0)
                    up(3)
                    down(1)
                    eng.wait_ge(x_updated, at(STAGE_D, i, p, 1, 1))
                    eng.wait_ge(xn_ready, at(STAGE_D, i, p, 1, 2))
                    fwd()
                    down(2)
                    down(3)
            eng.wait_ge(xTl_ready, NS * NB + 1)
            eng.wait_ge(acc_ready, NB * NS + 1)
            back(1)


SIGNS = np.zeros((P // 32, 4, HD, 2), np.float32)
SIGNS[:, 1, :, 0] = -1.0
SIGNS[:, 2, :, 1] = -1.0
SIGNS = SIGNS.reshape(P, 2)


def kernel(**inputs):
    import concourse.bacc as bacc
    from concourse.bass_utils import run_bass_kernel_spmd
    nc = bacc.Bacc("TRN2", target_bir_lowering=False, num_devices=1)
    g = {k: np.asarray(v) for k, v in inputs.items()}
    A, B, C, D = "L0_xattn_", "L0_ffn_", "L1_xattn_", "L1_ffn_"

    def head_rows(w):
        wt = w.T.reshape(P, NH, HD)
        return np.concatenate([wt, wt, wt, np.zeros_like(wt)], axis=2).reshape(P, -1)
    arrays = {
        "x": g["x"].reshape(-1, P),
        "ctxT": g["ctx_1024"].reshape(-1, P).T,
        "a_wg": g[A + "Wg"],
        "a_bg": np.broadcast_to(g[A + "bg"], (P, EA)),
        "a_w1": g[A + "W1"].transpose(1, 0, 2).reshape(P, -1),
        "a_b1": g[A + "b1"].reshape(-1, P).T,
        "a_w2": g[A + "W2"].reshape(EA, CA, P, P).transpose(2, 0, 1, 3).reshape(P, -1),
        "a_b2": g[A + "b2"].T,
        "b_wg": g[B + "Wg"].T,
        "b_w1": g[B + "W1"].transpose(2, 0, 1).reshape(P, -1),
        "b_b1": g[B + "b1"].T,
        "b_w3": g[B + "W3"].transpose(2, 0, 1).reshape(P, -1),
        "b_b3": g[B + "b3"].T,
        "b_w2": g[B + "W2"].transpose(2, 0, 1).reshape(P, -1),
        "b_b2": g[B + "b2"].T,
        "c_wqk": np.concatenate([head_rows(g[C + "Wq"]), head_rows(g[C + "Wk"])], axis=1),
        "c_wvo": np.concatenate([g[C + "Wv"].T, g[C + "Wo"].T], axis=1),
        "c_sign": SIGNS,
        "c_bv": np.broadcast_to(g[C + "bv"], (P, P)),
        "c_bo": g[C + "bo"].reshape(P, 1),
        "d_fc1": g[D + "fc1_q"],
        "d_fc2": g[D + "fc2_q"].reshape(CD, P, P).transpose(1, 0, 2).reshape(P, -1),
        "d_scales": np.concatenate([np.broadcast_to(g[D + "fc1_scales"].reshape(1, -1), (P, BT)),
                                    np.broadcast_to(g[D + "fc2_scales"].reshape(1, -1), (P, BT))], axis=1),
        "d_gamma": g[D + "ln_gamma"].reshape(P, 1),
        "d_beta": g[D + "ln_beta"].reshape(P, 1),
        "d_b1": g[D + "fc1_bias"].reshape(CD, P).T,
        "d_b2": g[D + "fc2_bias"].reshape(P, 1),
    }
    arrays = {k + "_in": np.ascontiguousarray(v) for k, v in arrays.items()}
    args = [nc.dram_tensor(k, v.shape, mybir.dt.from_np(v.dtype), kind="ExternalInput").ap() for k, v in arrays.items()]
    o = nc.dram_tensor("out", (NB * BT, P), F32, kind="ExternalOutput").ap()
    build(nc, *args, o)
    r = run_bass_kernel_spmd(nc, [arrays], core_ids=[0])
    return r.results[0]["out"].reshape(g["x"].shape)
```

```python
import numpy as np
import concourse.bass as bass
from concourse import mybir
from contextlib import ExitStack

F32 = mybir.dt.float32
F32R = mybir.dt.float32r
BF16 = mybir.dt.bfloat16
I32 = mybir.dt.int32
ALU = mybir.AluOpType
ACT = mybir.ActivationFunctionType
AX = mybir.AxisListType.X

P = 128
NB = 8
BT = 512
NT = BT // P
EPS = 1e-5

EA, FA = 8, 512
CA = FA // P
UA = EA * CA
EB = 16
NG = 4
CD = 4
ROUTE_SCALE = 2.5

NH, HD = 16, 8
HG = 4
SG = NH // HG
MASKED = -1e30

STAGE_A, STAGE_B, STAGE_C, STAGE_D = range(4)


def build(nc, x, ctxT, a_wg, a_bg, a_w1, a_b1, a_w2, a_b2,
          b_wg, b_w1, b_b1, b_w3, b_b3, b_w2, b_b2,
          c_wqk, c_wvo, c_sign, c_bv, c_bo, d_fc1, d_fc2, d_scales, d_gamma, d_beta, d_b1, d_b2, out):
    with ExitStack() as ctx:
        def sb(name, shape, dt=F32):
            return ctx.enter_context(nc.sbuf_tensor(name, shape, dt))

        def sem(name):
            return ctx.enter_context(nc.semaphore(name))

        hid_ps = [ctx.enter_context(nc.psum_tensor(f"hid_ps{k}", [P, BT], F32)) for k in range(4)]
        y_ps = [ctx.enter_context(nc.psum_tensor(f"y_ps{k}", [P, BT], F32)) for k in range(2)]
        cb_ps = ctx.enter_context(nc.psum_tensor("cb_ps", [P, BT], F32))
        tr_ps = ctx.enter_context(nc.psum_tensor("tr_ps", [P, BT], F32))

        weight_ps = [cb_ps, y_ps[1]]

        X = sb("X", [P, NB * BT])
        xn = sb("xn", [P, BT])
        xTh = sb("xTh", [P, 2, BT], F32R)
        xTl = sb("xTl", [P, 2, BT], F32R)
        accT = sb("accT", [P, 2, BT])
        ident = sb("ident", [P, P])
        st = sb("st", [P, NT, 6])
        mv = sb("mv", [P, NT, 2])
        carry = sb("carry", [P, 1])
        veps = sb("veps", [P, 2, NT])
        rstd = sb("rstd", [P, 2, NT])
        mhalf = sb("mhalf", [P, 2, NT])
        resid = sb("resid", [P, 2, NT])

        region1 = sb("region1", [P, 4 * EA * FA], F32R)
        region2 = sb("region2", [P, 4 * EB * P], F32R)

        def part(region, k, n, *dims):
            v = region[:, k * n:(k + 1) * n]
            if len(dims) < 2:
                return v
            names = [f"d{q}" for q in range(len(dims))]
            return v.rearrange(f"p ({' '.join(names)}) -> p {' '.join(names)}", **dict(zip(names, dims)))

        w1h, w1l = part(region1, 0, EA * FA, EA, FA), part(region1, 1, EA * FA, EA, FA)
        w2h, w2l = part(region1, 2, EA * FA, EA, CA, P), part(region1, 3, EA * FA, EA, CA, P)
        bw1h, bw1l = part(region2, 0, EB * P, EB, P), part(region2, 1, EB * P, EB, P)
        bw3h, bw3l = part(region2, 2, EB * P, EB, P), part(region2, 3, EB * P, EB, P)
        bw2h, bw2l = part(region1, 6, EB * P, EB, P), part(region1, 7, EB * P, EB, P)
        kdiag = [part(region1, k, NT * BT, NT, BT) for k in range(2)]
        qdiag = [part(region1, 2 + k, NT * BT, NT, BT) for k in range(2)]
        kp = part(region1, 4, 4 * BT, 4, BT)
        wqkh, wqkl = part(region2, 0, 2 * BT, 2, SG, P), part(region2, 1, 2 * BT, 2, SG, P)
        wvoh, wvol = part(region2, 10, 2 * P, 2, P), part(region2, 11, 2 * P, 2, P)
        fc1h, fc1l = part(region2, 6, BT), part(region2, 7, BT)
        fc2h, fc2l = part(region2, 8, BT, CD, P), part(region2, 9, BT, CD, P)
        raw = sb("raw", [P, 4, BT])

        hf = sb("hf", [P, 2, BT])
        hh = sb("hh", [P, 4, BT], F32R)
        hl = sb("hl", [P, 4, BT], F32R)
        wy = sb("wy", [P, 2, BT])
        cbs = sb("cbs", [P, 2, BT])
        sg = sb("sg", [P, 2, BT])
        combT = sb("combT", [2 * EB, 2, BT], F32R)
        sel = sb("sel", [2 * EB, EB, P], F32R)
        b1a, b2a = sb("b1a", [P, EA * CA]), sb("b2a", [P, EA])
        wga, bga = sb("wga", [P, EA]), sb("bga", [P, EA])
        b1b, b3b = sb("b1b", [P, EB]), sb("b3b", [P, EB])
        b2b = sb("b2b", [2 * EB, P])
        b2bh, b2bl = sb("b2bh", [2 * EB, P], F32R), sb("b2bl", [2 * EB, P], F32R)
        wgb = sb("wgb", [P, EB])
        wgbh, wgbl = sb("wgbh", [P, EB], F32R), sb("wgbl", [P, EB], F32R)
        ctxr = sb("ctxr", [P, 2, BT])
        TA = NB * NT
        TH = TA // 2
        lga = sb("lga", [P, TA, EA])
        combA = sb("combA", [P, TA, 2 * EA])
        lower = sb("lower", [P, EB, EB], BF16)
        upper = sb("upper", [P, EB, EB], BF16)
        rk1 = sb("rk1", [P, NT * EB * EB], BF16)
        rk2 = sb("rk2", [P, NT * EB * EB], BF16)
        rank = sb("rank", [P, TA, EA])
        mx = sb("mx", [P, TA])
        ex = wy[:, 1, 0:TA * EA].rearrange("p (t e) -> p t e", e=EA)
        ssum = sb("ssum", [P, TA])
        hi32 = wy[:, 0, 0:TA * EA].bitcast(F32R).rearrange("p (t e) -> p t e", e=EA)
        sgm = sb("sgm", [P, NT, EB])
        gmax, grank, gm1 = sb("gmax", [P, NT, NG]), sb("grank", [P, NT, NG]), sb("gm1", [P, NT, NG])
        hid4 = [hf[:, 0, :], hf[:, 1, :], wy[:, 0, :], wy[:, 1, :]]
        gate4 = [sg[:, 0, :], sg[:, 1, :], cbs[:, 0, :], cbs[:, 1, :]]
        qp = hl[:, 0:2, :]
        ah, al = hl[:, 2, :], hl[:, 3, :]
        ch, cl = hh[:, 0:2, :], hh[:, 2:4, :]
        prob = hid4
        VW = NT * NH * (HD + 1)
        vals = sb("vals", [P, 2, VW + 32])
        osb = sg[:, 0, :]
        sign = sb("sign", [P, 2])
        bvb, bo = sb("bvb", [P, P]), sb("bo", [P, 1])
        maskq, maskk = sb("maskq", [P, HG, P], BF16), sb("maskk", [P, HG, P], BF16)
        ident16 = sb("ident16", [P, P], BF16)
        selm = sb("selm", [2 * HG, HG, P], BF16)
        negmax = sb("negmax", [P, NT, HG])
        nm16 = sb("nm16", [P, NT, HG], BF16)
        nmb = sb("nmb", [P, NT, 2 * HG])
        nmT = sb("nmT", [2 * HG, 2, BT], BF16)
        rden = sb("rden", [P, NT, HG])
        gamma, beta = sb("gamma", [P, 1]), sb("beta", [P, 1])
        b1d, b2d = sb("b1d", [P, CD]), sb("b2d", [P, 1])
        msk = sb("msk", [P, NT, EB])
        rnk = sb("rnk", [P, NT, EB])
        wb = sb("wb", [P, NT, EB])
        wbh = sb("wbh", [P, NT, EB], F32R)
        combA_flat = combA[:].rearrange("p t e -> p (t e)")
        comb = sb("comb", [P, NT * 2 * EB])

        in_x0, in_x, in_small = sem("in_x0"), sem("in_x"), sem("in_small")
        in_raw = [sem(f"in_raw{k}") for k in range(4)]
        in_ctx = [sem(f"in_ctx{k}") for k in range(2)]
        consts, const_step = sem("consts"), sem("const_step")
        raw_hi, raw_lo = sem("raw_hi"), sem("raw_lo")
        logits_done, logits_read = sem("logits_done"), sem("logits_read")
        exp_in, exp_done, routed = sem("exp_in"), sem("exp_done"), sem("routed")
        selr = sem("selr")
        var_ready, rstd_ready, xn_ready = sem("var_ready"), sem("rstd_ready"), sem("xn_ready")
        xT_done, xTh_ready, xTl_ready = sem("xT_done"), sem("xTh_ready"), sem("xTl_ready")
        acc_ready, back_done, x_updated = sem("acc_ready"), sem("back_done"), sem("x_updated")
        dve = sem("dve")
        comb_ready = sem("comb_ready")
        combT_done, combT_ready = sem("combT_done"), sem("combT_ready")
        a_up, a_hf, a_hh, a_hl, a_down = sem("a_up"), sem("a_hf"), sem("a_hh"), sem("a_hl"), sem("a_down")
        a_hh_act, a_hl_pool = sem("a_hh_act"), sem("a_hl_pool")
        a_cb, a_cbs, a_wy, a_acc = sem("a_cb"), sem("a_cbs"), sem("a_wy"), sem("a_acc")
        stored = sem("stored")
        b_up1, b_up3, b_sg, b_hf, b_hh, b_hl = (sem(n) for n in ("b_up1", "b_up3", "b_sg", "b_hf", "b_hh", "b_hl"))
        b_down, b_cb, b_hw = (sem(n) for n in ("b_down", "b_cb", "b_hw"))
        c_proj, c_r, c_qk, c_kd, c_qd = (sem(n) for n in ("c_proj", "c_r", "c_qk", "c_kd", "c_qd"))
        c_s1, c_max, c_nm, c_nmt, c_nmT = (sem(n) for n in ("c_s1", "c_max", "c_nm", "c_nmt", "c_nmT"))
        c_s2, c_exp, c_pv, c_vp, c_v = (sem(n) for n in ("c_s2", "c_exp", "c_pv", "c_vp", "c_v"))
        c_osb, c_ott, c_kd_dve = sem("c_osb"), sem("c_ott"), sem("c_kd_dve")
        c_ch, c_cl, c_norm, c_ot, c_ah, c_al, c_wo = (sem(n) for n in ("c_ch", "c_cl", "c_norm", "c_ot", "c_ah", "c_al", "c_wo"))
        c_ctx = [sem(f"c_ctx{k}") for k in range(2)]
        in_scales, dequant, beta_done, diag_clear = sem("in_scales"), sem("dequant"), sem("beta_done"), sem("diag_clear")
        d_up, d_hf, d_hh, d_hl, d_down = (sem(n) for n in ("d_up", "d_hf", "d_hh", "d_hl", "d_down"))
        b_logits, b_sgm, wgb_split = sem("b_logits"), sem("b_sgm"), sem("wgb_split")
        bcomb_ready, bcombT_done, bcombT_ready = sem("bcomb_ready"), sem("bcombT_done"), sem("bcombT_ready")

        def blk(i, p, shift):
            return (i * 2 + (p + shift + NB)) % NB

        def at(stage, i, p, per_block, count):
            return i * (2 * per_block) + ((stage * NB + p) * per_block + count)

        def mm3(dst, wh, wl, xh, xl, start=True, stop=True):
            nc.tensor.matmul(dst, wh, xh, start=start, stop=False)
            nc.tensor.matmul(dst, wh, xl, start=False, stop=False)
            return nc.tensor.matmul(dst, wl, xh, start=False, stop=stop)

        class Chain:
            def __init__(self, eng):
                self.eng, self.base, self.n = eng, 0, 0

            def begin(self, i, p, per_block, start):
                self.per, self.n = per_block, 0
                self.base = i * (2 * per_block) + (start + p * per_block)

            def __call__(self, ins):
                ins.then_inc(dve, 1)
                self.n += 1
                self.eng.wait_ge(dve, self.base + self.n)

            def end(self):
                assert self.n == self.per, (self.n, self.per)

        HID, HF, HH, YB, CBB, HB = 4, 2, 4, 2, 1, 4

        NS = 4
        FIRST_SPLITS = 6
        X_AT = 10
        EXP_AT = 8
        LAST = CA - 1
        UV = EA * LAST
        DOWN_LAG = 3
        UP_AHEAD_A, UP_AHEAD_B = 3, 2
        block = ctx.enter_context(nc.Block())

        def flat(v):
            return v if len(v.shape) == 2 else v.rearrange(
                "p a b -> p (a b)" if len(v.shape) == 3 else "p a b c -> p (a b c)")

        raw_src = []
        for e in range(EA):
            raw_src.append((a_w1[:, e * FA:(e + 1) * FA], w1h[:, e, :], w1l[:, e, :]))
            raw_src.append((a_w2[:, e * FA:(e + 1) * FA], flat(w2h[:, e]), flat(w2l[:, e])))
        EQ = BT // P
        for src, wh, wl in ((b_w1, bw1h, bw1l), (b_w3, bw3h, bw3l)):
            for q in range(EB // EQ):
                raw_src.append((src[:, q * BT:(q + 1) * BT], flat(wh[:, q * EQ:(q + 1) * EQ]), flat(wl[:, q * EQ:(q + 1) * EQ])))
        NRAW0 = len(raw_src)
        for q in range(EB // EQ):
            raw_src.append((b_w2[:, q * BT:(q + 1) * BT], flat(bw2h[:, q * EQ:(q + 1) * EQ]), flat(bw2l[:, q * EQ:(q + 1) * EQ])))
        NRAW1 = len(raw_src)
        for q in range(2):
            raw_src.append((c_wqk[:, q * BT:(q + 1) * BT], flat(wqkh[:, q]), flat(wqkl[:, q])))
        raw_src.append((c_wvo, flat(wvoh), flat(wvol)))
        NRAW2 = len(raw_src)
        raw_src.append((d_fc1, fc1h, fc1l))
        raw_src.append((d_fc2, flat(fc2h), flat(fc2l)))
        NRAW = len(raw_src)

        SMALL = ((wga, a_wg), (bga, a_bg), (b1a, a_b1), (b2a, a_b2), (wgb, b_wg), (b1b, b_b1), (b3b, b_b3), (b2b, b_b2),
                 (sign, c_sign), (bvb, c_bv), (bo, c_bo), (gamma, d_gamma), (beta, d_beta), (b1d, d_b1), (b2d, d_b2))

        @block.sync
        def _(sp):
            for dst, src in SMALL:
                sp.dma_start(dst[:], src).then_inc(in_small, 16)
            for k in range(4):
                sp.dma_start(raw[:, k, :], raw_src[k][0]).then_inc(in_raw[k], 16)
            sp.dma_start(X[:, 0:BT].rearrange("p (t d) -> p t d", t=NT),
                         x[0:BT, :].rearrange("(t p) d -> p t d", p=P)).then_inc(in_x0, 16)
            sp.dma_start(ctxr[:, 0, :], ctxT[:, 0:BT]).then_inc(in_ctx[0], 16)
            sp.dma_start(X[:, BT:], ctxT[:, BT:]).then_inc(in_ctx[1], 16)

            def load_x(b):
                sp.dma_start(X[:, b * BT:(b + 1) * BT].rearrange("p (t d) -> p t d", t=NT),
                             x[b * BT:(b + 1) * BT, :].rearrange("(t p) d -> p t d", p=P)).then_inc(in_x, 16)
            for k in range(4, NRAW):
                if k == X_AT:
                    sp.wait_ge(logits_done, NB)
                if X_AT <= k < X_AT + NB - 1:
                    load_x(k - X_AT + 1)
                if k == NRAW - 1:
                    sp.wait_ge(b_hl, NB * EB + HB)
                    sp.dma_start(sg[:], d_scales.rearrange("p (k n) -> p k n", k=2)).then_inc(in_scales, 16)
                sp.wait_ge(raw_lo, k - 3)
                src = raw_src[k][0]
                dst = raw[:, k % 4, 0:src.shape[1]]
                sp.dma_start(dst if k < NRAW2 else dst.bitcast(I32), src).then_inc(in_raw[k % 4], 16)
            sp.dma_start(ctxr[:, 0, :], ctxT[:, 0:BT]).then_inc(c_ctx[0], 16)
            with sp.Fori(0, NB // 2) as i:
                for p in range(2):
                    sp.wait_ge(c_cl, at(0, i, p, 1, 1))
                    sp.dma_start(ctxr[:, 1 - p, :], ctxT[:, bass.ds(blk(i, p, 1) * BT, BT)]).then_inc(c_ctx[1 - p], 16)
            for b in range(NB):
                sp.wait_ge(x_updated, STAGE_D * NB + 2 + b)
                sp.dma_start(out[b * BT:(b + 1) * BT, :].rearrange("(t p) d -> p t d", p=P),
                             X[:, b * BT:(b + 1) * BT].rearrange("p (t d) -> p t d", t=NT)).then_inc(stored, 16)
            sp.wait_ge(stored, 16 * NB)

        @block.gpsimd
        def _(pool):
            g = nc.gpsimd
            n = 0

            def step(ins):
                nonlocal n
                ins.then_inc(const_step, 1)
                n += 1
                pool.wait_ge(const_step, n)
            g.memset(mhalf[:], -0.5)
            g.memset(accT[:, 1, :], 0.0).then_inc(acc_ready, 1)
            step(g.memset(ident[:], 0.0))
            step(g.affine_select(out=ident[:], in_=ident[:], compare_op=ALU.not_equal, fill=1.0, base=0,
                                 pattern=[[-1, P]], channel_multiplier=1))
            step(g.memset(lower[:], 1.0))
            step(g.memset(upper[:], 1.0))
            step(g.affine_select(out=lower[:], in_=lower[:], compare_op=ALU.is_gt, fill=0.0, base=0,
                                 pattern=[[1, EB], [-1, EB]], channel_multiplier=0))
            step(g.affine_select(out=upper[:], in_=upper[:], compare_op=ALU.is_ge, fill=0.0, base=0,
                                 pattern=[[-1, EB], [1, EB]], channel_multiplier=0))
            step(g.memset(maskq[:], 0.0))
            step(g.memset(maskk[:], 0.0))
            step(g.affine_select(out=maskq[:], in_=maskq[:], compare_op=ALU.is_gt, fill=MASKED, base=0,
                                 pattern=[[0, HG], [-1, P]], channel_multiplier=1))
            step(g.affine_select(out=maskk[:], in_=maskk[:], compare_op=ALU.is_gt, fill=MASKED, base=0,
                                 pattern=[[0, HG], [1, P]], channel_multiplier=-1))
            g.memset(maskq[0:1, :, 0:1], 0.0)
            g.memset(maskk[0:1, :, 0:1], 0.0)
            g.memset(vals[:], 1.0)
            g.memset(veps[:], 1.0).then_inc(consts, 1)

            def rstd_step(stage, i, p):
                pool.wait_ge(var_ready, at(stage, i, p, 1, 2))
                g.tensor_tensor(rstd[:], veps[:], mhalf[:], ALU.pow).then_inc(rstd_ready, 1)

            pool.sem_inc(b_hl, HB)
            pool.sem_inc(a_hl_pool, 1)
            pool.wait_ge(var_ready, 1)
            g.tensor_tensor(rstd[:], veps[:], mhalf[:], ALU.pow).then_inc(rstd_ready, 1)

            with pool.Fori(0, NB // 2) as i:
                for p in range(2):
                    def add(e):
                        pool.wait_ge(a_wy, at(0, i, p, EA, e + 1 + YB))
                        if e > 1:
                            pool.wait_ge(a_acc, at(0, i, p, EA - 2, e - 1))
                        g.tensor_tensor(accT[:, p, :], accT[:, p, :], wy[:, e % 2, :],
                                        ALU.add).then_inc(a_acc if e < EA - 1 else acc_ready, 1)
                    for e in range(EA):
                        u = e * CA + LAST
                        pool.wait_ge(a_hh_act, at(0, i, p, EA, e + 1))
                        pool.wait_ge(a_down, at(0, i, p, UA, u + 1))
                        g.tensor_tensor(hl[:, u % 4, :], hf[:, u % 2, :], hh[:, u % 4, :].bitcast(F32),
                                        ALU.subtract).then_inc(a_hl_pool, 1)
                        if e >= 2:
                            add(e - 1)
                        if e == 2:
                            rstd_step(STAGE_A, i, p)
                    add(EA - 1)
            pool.wait_ge(a_down, NB * UA + HH)
            g.memset(region1[:, 0:4 * NT * BT].bitcast(F32), 0.0).then_inc(diag_clear, 1)
            with pool.Fori(0, NB // 2) as i:
                for p in range(2):
                    for e in range(EB):
                        pool.wait_ge(b_hh, at(0, i, p, EB, e + 1))
                        pool.wait_ge(b_down, at(0, i, p, EB, e + 1))
                        g.tensor_tensor(hl[:, e % 4, :], hid4[e % 4], hh[:, e % 4, :].bitcast(F32),
                                        ALU.subtract).then_inc(b_hl, 1)
                        if e == 1:
                            rstd_step(STAGE_B, i, p)
            for stage in (STAGE_C, STAGE_D):
                with pool.Fori(0, NB // 2) as i:
                    for p in range(2):
                        rstd_step(stage, i, p)

        def ln_stats(eng, link, off, first=None):
            for t in range(NT):
                ins = nc.vector.bn_stats(st[:, t, :], X[:, bass.ds(off + t * P, P)])
            link(ins)
            nc.vector.memset(carry[:], 0.0)
            for t in range(NT):
                ins = nc.vector.bn_aggr(mv[:, t, :], st[:, t, :])
            link(ins)
            link(nc.vector.tensor_scalar_add(veps[:, 0, :], mv[:, :, 1], EPS))
            nc.vector.scalar_tensor_tensor(veps[:, 1, :], veps[:, 0, :], EPS, mv[:, :, 1],
                                           op0=ALU.mult, op1=ALU.add).then_inc(var_ready, 1)

        def ln_apply(off, twice=0):
            for t in range(NT):
                ins = nc.vector.tensor_scalar(xn[:, t * P:(t + 1) * P], X[:, bass.ds(off + t * P, P)],
                                              mv[:, t, 0:1], rstd[:, twice, t:t + 1], ALU.subtract, ALU.mult)
            ins.then_inc(xn_ready, 1)

        def spread(v, *dims):
            return bass.AP(v.tensor, v.offset, [list(v.ap[0])] + [list(d) for d in dims])

        def rank_of(link, vals, T, E, dst):
            for step in rank_steps(link, vals, T, E, dst):
                step()

        def rank_steps(link, vals, T, E, dst):
            own = spread(vals, [E, T], [1, E], [0, E])
            other = spread(vals, [E, T], [0, E], [1, E])
            low, upp = (spread(m[:], [0, T], [EB, E], [1, E]) for m in (lower, upper))
            r1, r2 = (m[:, 0:T * E * E].rearrange("p (t e j) -> p t e j", t=T, e=E) for m in (rk1, rk2))
            v = nc.vector

            def compare_ge():
                link(v.tensor_tensor(r1, other, own, ALU.is_ge))

            def compare_gt():
                link(v.tensor_tensor(r2, other, own, ALU.is_gt))

            def select():
                v.tensor_tensor(r1, r1, low, ALU.mult)
                link(v.tensor_tensor(r2, r2, upp, ALU.mult))

            def count():
                link(v.tensor_tensor(r1, r1, r2, ALU.add))
                link(v.tensor_reduce(dst, r1, AX, ALU.add))
            return compare_ge, compare_gt, select, count
        RANK_LINKS = 5

        def write_back(eng, stage, i, p):
            eng.wait_ge(back_done, at(stage, i, p, 1, 1))
            xs = X[:, bass.ds(blk(i, p, -1) * BT, BT)]
            nc.vector.tensor_tensor(xs, xs, tr_ps[:], ALU.add).then_inc(x_updated, 1)
            eng.wait_ge(x_updated, at(stage, i, p, 1, 1))

        def apply_next(eng, stage, i, p, twice=0):
            eng.wait_ge(rstd_ready, at(stage, i, p, 1, 2))
            ln_apply(blk(i, p, 1) * BT, twice)

        def low_next(eng, stage, i, p, extra=0):
            eng.wait_ge(xTh_ready, at(stage, i, p, 1, 2 + extra))
            nc.vector.tensor_tensor(xTl[:, 1 - p, :], tr_ps[:], xTh[:, 1 - p, :].bitcast(F32),
                                    ALU.subtract).then_inc(xTl_ready, 1)

        def high_next(eng, stage, i, p, extra=0):
            eng.wait_ge(xT_done, at(stage, i, p, 1, 2 + extra))
            nc.scalar.activation(xTh[:, 1 - p, :], tr_ps[:], ACT.Copy).then_inc(xTh_ready, 1)


        @block.vector
        def _(eng):
            v = nc.vector
            link = Chain(eng)
            link.per, link.n, link.base = 10 ** 6, 0, 0
            eng.sem_inc(a_hl, LAST)
            eng.sem_inc(a_wy, YB)
            eng.sem_inc(b_hf, 2)
            eng.sem_inc(c_max, 2)
            eng.sem_inc(c_al, 1)
            eng.sem_inc(d_hl, 2)
            eng.sem_inc(b_hw, 2)
            eng.wait_ge(consts, 1)
            eng.wait_ge(in_x0, 16)
            ln_stats(eng, link, 0)
            def split_low(k):
                eng.wait_ge(raw_hi, k + 1)
                src, wh, wl = raw_src[k]
                v.tensor_tensor(wl, raw[:, k % 4, 0:src.shape[1]], wh.bitcast(F32), ALU.subtract).then_inc(raw_lo, 1)

            def selector(E):
                return v.tensor_tensor(sel[0:2 * E, 0:E, :], spread(ident[0:2 * E, 0:E], [1, E], [0, P]),
                                       spread(ident[0:2 * E, E:2 * E], [1, E], [0, P]), ALU.add)
            for k in range(FIRST_SPLITS):
                split_low(k)
                if k == 1:
                    eng.wait_ge(rstd_ready, 1)
                    ln_apply(0)
                if k == 5:
                    eng.wait_ge(xTh_ready, 1)
                    v.tensor_tensor(xTl[:, 0, :], tr_ps[:], xTh[:, 0, :].bitcast(F32), ALU.subtract).then_inc(xTl_ready, 1)
            selector(EA).then_inc(selr, 1)
            eng.wait_ge(logits_done, NB)
            eng.wait_ge(in_small, 16 * len(SMALL))
            lgp = cb_ps[:, 0:TA * EA].rearrange("p (t e) -> p t e", e=EA)
            link(v.tensor_tensor(lga[:], lgp, spread(bga[:], [0, TA], [1, EA]), ALU.add))
            link(v.tensor_reduce(mx[:], lga[:], AX, ALU.max))
            v.tensor_tensor(ex[:], lga[:], spread(mx[:], [1, TA], [0, EA]), ALU.subtract).then_inc(exp_in, 1)
            k = FIRST_SPLITS
            for t0 in range(0, TA, TH):
                for step in rank_steps(link, lga[:, t0:t0 + TH, :], TH, EA, rank[:, t0:t0 + TH, :]):
                    step()
                    split_low(k)
                    k += 1
            link(v.tensor_scalar(rank[:], rank[:], 1.5, None, ALU.is_lt))
            eng.wait_ge(exp_done, 1)
            link(v.tensor_tensor(ex[:], ex[:], rank[:], ALU.mult))
            link(v.tensor_reduce(ssum[:], ex[:], AX, ALU.add))
            link(v.reciprocal(ssum[:], ssum[:]))
            link(v.tensor_tensor(ex[:], ex[:], spread(ssum[:], [1, TA], [0, EA]), ALU.mult))
            link(v.tensor_copy(hi32[:], ex[:]))
            v.tensor_copy(combA[:, :, 0:EA], hi32[:].bitcast(F32))
            v.tensor_tensor(combA[:, :, EA:2 * EA], ex[:], hi32[:].bitcast(F32), ALU.subtract).then_inc(routed, 1)
            for k in range(k, NRAW0):
                split_low(k)
            eng.wait_ge(in_x, 16 * (NB - 1))
            start = link.n

            with eng.Fori(0, NB // 2) as i:
                for p in range(2):
                    link.begin(i, p, 3, start)

                    def weigh(e):
                        eng.wait_ge(a_down, at(0, i, p, UA, (e + 1) * CA + HH))
                        eng.wait_ge(a_cbs, at(0, i, p, EA, e + 1 + CBB))
                        if e >= 3:
                            eng.wait_ge(a_acc, at(0, i, p, EA - 2, e - 2))
                        elif e:
                            eng.wait_ge(acc_ready, at(STAGE_A, i, p, 1, 1))
                        dst = accT[:, p, :] if e == 0 else wy[:, e % 2, :]
                        v.scalar_tensor_tensor(dst, y_ps[e % 2][:], b2a[:, e:e + 1], cbs[:, e % 2, :],
                                               op0=ALU.add, op1=ALU.mult).then_inc(a_wy, 1)
                    for u in range(UA):
                        e, c = divmod(u, CA)
                        if c < LAST:
                            eng.wait_ge(a_hf, at(0, i, p, UA, u + 1 + HID))
                            eng.wait_ge(a_down, at(0, i, p, UA, u + 1))
                            v.tensor_copy(hh[:, u % 4, :], hf[:, u % 2, :]).then_inc(a_hh, 1)
                            eng.wait_ge(a_hh, at(0, i, p, UV, e * LAST + c + 1))
                            v.tensor_tensor(hl[:, u % 4, :], hf[:, u % 2, :], hh[:, u % 4, :].bitcast(F32),
                                            ALU.subtract).then_inc(a_hl, 1)
                        if u == 5:
                            write_back(eng, STAGE_A, i, p)
                        if u == 8:
                            ln_stats(eng, link, blk(i, p, 1) * BT)
                        if u == 13:
                            apply_next(eng, STAGE_A, i, p)
                        if u == 19:
                            low_next(eng, STAGE_A, i, p)
                        if u % CA == CA - 1 and u > CA:
                            weigh(u // CA - 1)
                    weigh(EA - 1)
                    link.end()
            start += NB * 3

            for k in range(NRAW0, NRAW1):
                split_low(k)
            link.per, link.n, link.base = 10 ** 6, 0, start
            link(v.tensor_copy(wgbh[:], wgb[:]))
            v.tensor_tensor(wgbl[:], wgb[:], wgbh[:].bitcast(F32), ALU.subtract).then_inc(wgb_split, 1)
            link(v.tensor_copy(b2bh[:], b2b[:]))
            v.tensor_tensor(b2bl[:], b2b[:], b2bh[:].bitcast(F32), ALU.subtract)
            selector(EB).then_inc(selr, 1)

            def choose_groups(link):
                link(v.tensor_reduce(gmax[:], spread(sgm[:], [EB // NG, NT * NG], [1, EB // NG]), AX, ALU.max))
                rank_of(link, gmax[:], NT, NG, grank[:])
                link(v.tensor_scalar(grank[:], grank[:], 1.5, None, ALU.is_lt))
                v.tensor_scalar_add(gm1[:], grank[:], -1.0)
                each = [1, NT * NG], [0, EB // NG]
                m = spread(msk[:], [EB // NG, NT * NG], [1, EB // NG])
                link(v.tensor_tensor(m, spread(sgm[:], [EB // NG, NT * NG], [1, EB // NG]), spread(grank[:], *each), ALU.mult))
                link(v.tensor_tensor(m, m, spread(gm1[:], *each), ALU.add))


            def route_weights(link):
                link(v.tensor_scalar(rnk[:], rnk[:], 3.5, None, ALU.is_lt))
                link(v.tensor_tensor(wb[:], sgm[:], rnk[:], ALU.mult))
                link(v.tensor_reduce(ssum[:, 0:NT], wb[:], AX, ALU.add))
                link(v.reciprocal(ssum[:, 0:NT], ssum[:, 0:NT]))
                link(v.tensor_tensor(wb[:], wb[:], spread(ssum[:], [1, NT], [0, EB]), ALU.mult))
                link(v.tensor_scalar(wb[:], wb[:], ROUTE_SCALE, None, ALU.mult))
                link(v.tensor_copy(wbh[:], wb[:]))
                rows = comb[:].rearrange("p (t s e) -> p t s e", t=NT, s=2)
                v.tensor_copy(rows[:, :, 0, :], wbh[:].bitcast(F32))
                v.tensor_tensor(rows[:, :, 1, :], wb[:], wbh[:].bitcast(F32), ALU.subtract).then_inc(bcomb_ready, 1)
            eng.wait_ge(b_sgm, 1)
            choose_groups(link)
            rank_of(link, msk[:], NT, EB, rnk[:])
            route_weights(link)
            start += link.n

            eng.wait_ge(acc_ready, STAGE_B * NB + 1)
            with eng.Fori(0, NB // 2) as i:
                for p in range(2):
                    link.begin(i, p, 3 + 4 + 2 * RANK_LINKS + 7, start)
                    ranking = rank_steps(link, msk[:], NT, EB, rnk[:])
                    for e in range(EB):
                        eng.wait_ge(b_sg, at(0, i, p, EB, e + 1 + 2))
                        eng.wait_ge(b_up3, at(0, i, p, EB, e + 1))
                        eng.wait_ge(b_hl, at(0, i, p, EB, e + 1))
                        v.scalar_tensor_tensor(hid4[e % 4], hid_ps[2 + e % 2][:], b3b[:, e:e + 1], gate4[e % 4],
                                               op0=ALU.add, op1=ALU.mult).then_inc(b_hf, 1)
                        eng.wait_ge(b_hf, at(0, i, p, EB, e + 1 + 2))
                        eng.wait_ge(b_cb, at(0, i, p, EB, e + 1))
                        v.tensor_tensor(hid4[e % 4], hid4[e % 4], weight_ps[e % 2][:], ALU.mult).then_inc(b_hw, 1)
                        if e == 1:
                            write_back(eng, STAGE_B, i, p)
                        if e == 2:
                            ln_stats(eng, link, blk(i, p, 1) * BT)
                        if e == 4:
                            apply_next(eng, STAGE_B, i, p)
                        if e == 6:
                            low_next(eng, STAGE_B, i, p)
                        if e == 9:
                            eng.wait_ge(b_sgm, at(0, i, p, 1, 2))
                            choose_groups(link)
                        if 10 <= e < 14:
                            ranking[e - 10]()
                        if e == 14:
                            eng.wait_ge(bcombT_done, at(0, i, p, 1, 1))
                            route_weights(link)
                    link.end()
            start += NB * link.per

            link.per, link.n, link.base = 10 ** 6, 0, start
            for k in range(NRAW1, NRAW2):
                split_low(k)
            eng.wait_ge(in_scales, 16)
            for k in (NRAW2, NRAW2 + 1):
                eng.wait_ge(in_raw[k % 4], 16 * (k // 4 + 1))
                slot = raw[:, k % 4, :]
                v.scalar_tensor_tensor(slot, slot.bitcast(I32), -128.0, sg[:, k - NRAW2, :],
                                       op0=ALU.add, op1=ALU.mult).then_inc(dequant, 1)
            eng.wait_ge(beta_done, 1)
            slot = raw[:, NRAW2 % 4, :]
            v.tensor_scalar(slot, slot, gamma[:, 0:1], None, ALU.mult).then_inc(dequant, 1)
            v.tensor_tensor(b1d[:], b1d[:], cb_ps[:, 0:CD], ALU.add).then_inc(dequant, 1)
            for k in range(NRAW2, NRAW):
                split_low(k)
            v.tensor_copy(ident16[:], ident[:])
            v.tensor_tensor(selm[:], spread(ident[0:2 * HG, 0:HG], [1, HG], [0, P]),
                            spread(ident[0:2 * HG, HG:2 * HG], [1, HG], [0, P]), ALU.add).then_inc(selr, 1)

            def at4(i, p, g, ahead, per_step, count):
                return i * (2 * SG * per_step) + ((p * SG + g + ahead) * per_step + count)

            def max_of(i, p, g, b):
                eng.wait_ge(c_s1, at4(i, p, g, 1, NT, b + 1))
                v.tensor_reduce(negmax[:, b, :], hid_ps[b % 2][:].rearrange("p (i k) -> p i k", i=HG), AX, ALU.max,
                                negate=True).then_inc(c_max, 1)

            def split_max(i, p, g):
                eng.wait_ge(c_max, at4(i, p, g, 1, NT, NT + 2))
                link(v.tensor_copy(nm16[:], negmax[:]))
                v.tensor_copy(nmb[:, :, 0:HG], nm16[:])
                v.tensor_tensor(nmb[:, :, HG:], negmax[:], nm16[:], ALU.subtract).then_inc(c_nm, 1)

            def pack(i, p, g, which, bank=cb_ps):
                eng.wait_ge(c_r, at4(i, p, g, 2, 2, which + 1))
                dst = kp[:, (g + 2) % 4, :] if which else qp[:, g % 2, :]
                v.scalar_tensor_tensor(dst, cbs[:, which, :], sign[:, which:which + 1], bank[:],
                                       op0=ALU.mult, op1=ALU.add).then_inc(c_qk, 1)

            def spread_k(i, p, g):
                eng.wait_ge(c_qk, at4(i, p, g, 2, 2, 2))
                for h in range(HG // 2, HG):
                    rows = slice(32 * h, 32 * h + 32)
                    ins = v.tensor_copy(kdiag[g % 2][rows, :, h * P:(h + 1) * P],
                                        kp[rows, (g + 2) % 4, :].rearrange("p (b k) -> p b k", b=NT))
                ins.then_inc(c_kd_dve, 1)

            def spread_q(i, p, g):
                eng.wait_ge(c_qk, at4(i, p, g, 2, 2, 1))
                for h in range(HG):
                    rows = slice(32 * h, 32 * h + 32)
                    ins = v.tensor_copy(qdiag[g % 2][rows, :, h * P:(h + 1) * P],
                                        qp[rows, g % 2, :].rearrange("p (b k) -> p b k", b=NT))
                ins.then_inc(c_qd, 1)

            def values(par, n):
                eng.wait_ge(c_vp, n)
                dst = vals[:, par, 0:VW].rearrange("p (b h d) -> p b h d", b=NT, h=NH)[:, :, :, 0:HD]
                v.tensor_tensor(dst, cb_ps[:].rearrange("p (b h d) -> p b h d", b=NT, h=NH),
                                spread(bvb[:], [0, NT], [HD, NH], [1, HD]), ALU.add).then_inc(c_v, 1)

            def normalise(i, p, g):
                eng.wait_ge(c_ott, at4(i, p, g, 0, 1, 1))
                rows = tr_ps[:].rearrange("p (b i r) -> p b i r", b=NT, i=HG)
                link(v.reciprocal(rden[:], rows[:, :, :, HD]))
                dst = spread(xn[:, g * HG * HD:], [P, NT], [HD, HG], [1, HD])
                v.tensor_tensor(dst, rows[:, :, :, 0:HD], spread(rden[:], [HG, NT], [1, HG], [0, HD]),
                                ALU.mult).then_inc(c_norm, 1)

            def ctx_low(par, n):
                eng.wait_ge(c_ch, n)
                v.tensor_tensor(cl[:, par, :], ctxr[:, par, :], ch[:, par, :].bitcast(F32), ALU.subtract).then_inc(c_cl, 1)
            ctx_low(0, 1)
            eng.wait_ge(diag_clear, 1)
            for g in (-2, -1):
                pack(0, 0, g, 0)
                pack(0, 0, g, 1, y_ps[g % 2])
                spread_k(0, 0, g)
                spread_q(0, 0, g)
            values(0, 1)
            for b in range(NT):
                max_of(0, 0, -1, b)
            split_max(0, 0, -1)
            start += link.n

            with eng.Fori(0, NB // 2) as i:
                for p in range(2):
                    link.begin(i, p, 3 + SG + SG, start)
                    for g in range(SG):
                        for b in range(NT):
                            max_of(i, p, g, b)
                            if g == 0 and b == 1:
                                write_back(eng, STAGE_C, i, p)
                                ctx_low(1 - p, at(0, i, p, 1, 2))
                            if g == 1 and b == 1:
                                low_next(eng, STAGE_C, i, p)
                            if b == 2:
                                pack(i, p, g, 0)
                                pack(i, p, g, 1, y_ps[(g + 1) % 2])
                                spread_k(i, p, g)
                        eng.wait_ge(c_nmt, at4(i, p, g, 0, 1, 1))
                        split_max(i, p, g)
                        if g:
                            normalise(i, p, g - 1)
                        eng.wait_ge(c_s2, at4(i, p, g, 0, NT, NT))
                        spread_q(i, p, g)
                        if g == SG - 1:
                            normalise(i, p, g)
                            eng.wait_ge(c_ah, at(0, i, p, 1, 1))
                            v.tensor_tensor(al, tr_ps[:], ah.bitcast(F32), ALU.subtract).then_inc(c_al, 1)
                        if g == 0:
                            ln_stats(eng, link, blk(i, p, 1) * BT)
                            apply_next(eng, STAGE_C, i, p)
                        if g == 2:
                            values(1 - p, at(0, i, p, 1, 2))
                    link.end()
            start += NB * link.per

            eng.wait_ge(rstd_ready, STAGE_D * NB + 1)
            ln_apply(0, 1)
            eng.wait_ge(xTh_ready, STAGE_D * NB + 2)
            v.tensor_tensor(xTl[:, 0, :], tr_ps[:], xTh[:, 0, :].bitcast(F32), ALU.subtract).then_inc(xTl_ready, 1)
            with eng.Fori(0, NB // 2) as i:
                for p in range(2):
                    link.begin(i, p, 4, start)

                    def low(c):
                        eng.wait_ge(d_hh, at(0, i, p, CD, c + 1))
                        v.tensor_tensor(hl[:, c, :], hf[:, c % 2, :], hh[:, c, :].bitcast(F32), ALU.subtract).then_inc(d_hl, 1)
                    v.tensor_scalar_add(resid[:, 0, :], rstd[:, 0, :], 1.0)
                    link(v.scalar_tensor_tensor(resid[:, 1, :], mv[:, :, 0], -1.0, rstd[:, 0, :], op0=ALU.mult, op1=ALU.mult))
                    for k in range(NT):
                        xs = X[:, bass.ds((i * 2 + p) * BT + k * P, P)]
                        v.tensor_scalar(xs, xs, resid[:, 0, k:k + 1], resid[:, 1, k:k + 1], ALU.mult, ALU.add)
                    ln_stats(eng, link, blk(i, p, 1) * BT)
                    low(0)
                    write_back(eng, STAGE_D, i, p)
                    low(1)
                    apply_next(eng, STAGE_D, i, p, 1)
                    low(2)
                    low(3)
                    low_next(eng, STAGE_D, i, p, 1)
                    eng.wait_ge(d_down, at(0, i, p, CD, CD + 4))
                    v.tensor_scalar(accT[:, p, :], y_ps[p][:], b2d[:, 0:1], 0.5, ALU.add, ALU.mult).then_inc(acc_ready, 1)
                    link.end()
            eng.wait_ge(back_done, NB * NS + 1)
            xs = X[:, (NB - 1) * BT:]
            v.tensor_tensor(xs, xs, tr_ps[:], ALU.add).then_inc(x_updated, 1)

        @block.scalar
        def _(eng):
            a = nc.scalar
            eng.sem_inc(a_hf, HID)
            eng.sem_inc(a_cbs, CBB)
            eng.sem_inc(b_sg, 2)

            eng.sem_inc(c_exp, 2)
            eng.sem_inc(c_osb, 1)
            eng.sem_inc(d_hf, 4)

            def split_high(k):
                eng.wait_ge(in_raw[k % 4], 16 * (k // 4 + 1))
                src, wh, _ = raw_src[k]
                a.activation(wh, raw[:, k % 4, 0:src.shape[1]], ACT.Copy).then_inc(raw_hi, 1)
            for k in range(NRAW0):
                if k == EXP_AT:
                    eng.wait_ge(exp_in, 1)
                    a.activation(ex[:], ex[:], ACT.Exp).then_inc(exp_done, 1)
                split_high(k)
                if k == NRAW0 - 5:
                    eng.wait_ge(routed, 1)
                    a.activation(comb[:, 0:NT * 2 * EA], combA_flat[:, 0:NT * 2 * EA], ACT.Copy).then_inc(comb_ready, 1)
                if k == 4:
                    eng.wait_ge(xT_done, 1)
                    a.activation(xTh[:, 0, :], tr_ps[:], ACT.Copy).then_inc(xTh_ready, 1)
            eng.wait_ge(combT_done, 1)
            a.activation(combT[0:2 * EA, 0, :], tr_ps[0:2 * EA, :], ACT.Copy).then_inc(combT_ready, 1)

            with eng.Fori(0, NB // 2) as i:
                for p in range(2):
                    for u in range(UA):
                        e, c = divmod(u, CA)
                        eng.wait_ge(a_up, at(0, i, p, UA, u + 1))
                        if c == 1:
                            eng.wait_ge(a_hl_pool, at(0, i, p, EA, e + 1))
                        else:
                            eng.wait_ge(a_hl, at(0, i, p, UV, e * LAST + max(c - 1, 0) + LAST))
                        a.activation(hf[:, u % 2, :], hid_ps[u % 4][:], ACT.Relu,
                                     bias=b1a[:, u:u + 1]).then_inc(a_hf, 1)
                        if c == LAST:
                            eng.wait_ge(a_hf, at(0, i, p, UA, u + 1 + HID))
                            eng.wait_ge(a_down, at(0, i, p, UA, u + 1))
                            a.activation(hh[:, u % 4, :], hf[:, u % 2, :], ACT.Copy).then_inc(a_hh_act, 1)
                        if u % CA == 2:
                            e = u // CA
                            eng.wait_ge(a_cb, at(0, i, p, EA, e + 1))
                            eng.wait_ge(a_wy, at(0, i, p, EA, e + 1))
                            a.activation(cbs[:, e % 2, :], cb_ps[:], ACT.Copy).then_inc(a_cbs, 1)
                        if u == 18:
                            high_next(eng, STAGE_A, i, p)
                        if u == 20:
                            eng.wait_ge(combT_ready, at(0, i, p, 1, 1))
                            a.activation(comb[:, 0:NT * 2 * EA],
                                         combA_flat[:, bass.ds(blk(i, p, 1) * (NT * 2 * EA), NT * 2 * EA)],
                                         ACT.Copy).then_inc(comb_ready, 1)
                        if u == 26:
                            eng.wait_ge(combT_done, at(0, i, p, 1, 2))
                            a.activation(combT[0:2 * EA, 1 - p, :], tr_ps[0:2 * EA, :], ACT.Copy).then_inc(combT_ready, 1)

            eng.wait_ge(a_down, NB * UA + HH)
            for k in range(NRAW0, NRAW1):
                split_high(k)

            def scores(n):
                eng.wait_ge(b_logits, n)
                a.activation(sgm[:].rearrange("p t e -> p (t e)"), tr_ps[:, 0:NT * EB], ACT.Sigmoid).then_inc(b_sgm, 1)
            scores(1)
            eng.wait_ge(acc_ready, STAGE_B * NB + 1)
            eng.wait_ge(bcombT_done, 1)
            a.activation(combT[:, 0, :], tr_ps[0:2 * EB, :], ACT.Copy).then_inc(bcombT_ready, 1)
            with eng.Fori(0, NB // 2) as i:
                for p in range(2):
                    def high(e):
                        eng.wait_ge(b_hw, at(0, i, p, EB, e + 1 + 2))
                        eng.wait_ge(b_down, at(0, i, p, EB, e + 1))
                        a.activation(hh[:, e % 4, :], hid4[e % 4], ACT.Copy).then_inc(b_hh, 1)
                    for e in range(EB):
                        if e >= 2:
                            high(e - 2)
                        eng.wait_ge(b_up1, at(0, i, p, EB, e + 1))
                        a.activation(gate4[e % 4], hid_ps[e % 2][:], ACT.Silu, bias=b1b[:, e:e + 1]).then_inc(b_sg, 1)
                        if e == 6:
                            high_next(eng, STAGE_B, i, p)
                        if e == 8:
                            scores(at(0, i, p, 1, 2))
                    high(EB - 2)
                    eng.wait_ge(bcombT_done, at(0, i, p, 1, 2))
                    a.activation(combT[:, 1 - p, :], tr_ps[0:2 * EB, :], ACT.Copy).then_inc(bcombT_ready, 1)
                    high(EB - 1)
                    eng.wait_ge(b_down, at(0, i, p, EB, EB + HH))
                    a.activation(accT[:, p, :], y_ps[0][:], ACT.Copy).then_inc(acc_ready, 1)

            eng.wait_ge(b_down, NB * EB + HH)
            for k in range(NRAW1, NRAW2):
                split_high(k)
            eng.wait_ge(dequant, 3)
            for k in range(NRAW2, NRAW):
                split_high(k)

            def at4(i, p, g, ahead, per_step, count):
                return i * (2 * SG * per_step) + ((p * SG + g + ahead) * per_step + count)

            def ctx_high(par, arrived):
                eng.wait_ge(c_ctx[par], arrived)
                a.activation(ch[:, par, :], ctxr[:, par, :], ACT.Copy).then_inc(c_ch, 1)

            def rounded(i, p, g, which, bank=cb_ps):
                eng.wait_ge(c_proj, at4(i, p, g, 2, 2, which + 1))
                if not (isinstance(i, int) and g == -2):
                    eng.wait_ge(c_qk, at4(i, p, g, 1, 2, which + 1))
                a.activation(cbs[:, which, :].bitcast(F32R), bank[:], ACT.Copy).then_inc(c_r, 1)

            def spread_k(i, p, g):
                eng.wait_ge(c_qk, at4(i, p, g, 2, 2, 2))
                for h in range(HG // 2):
                    rows = slice(32 * h, 32 * h + 32)
                    ins = a.activation(kdiag[g % 2][rows, :, h * P:(h + 1) * P],
                                       kp[rows, (g + 2) % 4, :].bitcast(F32).rearrange("p (b k) -> p b k", b=NT), ACT.Copy)
                ins.then_inc(c_kd, 1)

            def shifts(i, p, g):
                eng.wait_ge(c_nmt, at4(i, p, g, 1, 1, 1))
                a.activation(nmT[:, (g + 1) % 2, :], tr_ps[0:2 * HG, :], ACT.Copy).then_inc(c_nmT, 1)
            ctx_high(0, 16)
            eng.wait_ge(diag_clear, 1)
            for g in (-2, -1):
                rounded(0, 0, g, 0)
                rounded(0, 0, g, 1, y_ps[g % 2])
                spread_k(0, 0, g)
            shifts(0, 0, -1)
            with eng.Fori(0, NB // 2) as i:
                for p in range(2):
                    for g in range(SG):
                        for b in range(NT):
                            eng.wait_ge(c_s2, at4(i, p, g, 0, NT, b + 1))
                            eng.wait_ge(c_pv, at4(i, p, g, 0, NT, b + 1))
                            a.activation(prob[b], hid_ps[2 + b % 2][:], ACT.Exp, scale=float(HD) ** -0.5).then_inc(c_exp, 1)
                            if b == 1:
                                rounded(i, p, g, 0)
                                rounded(i, p, g, 1, y_ps[(g + 1) % 2])
                            if g == 0 and b == 1:
                                ctx_high(1 - p, i * 16 + 16 if p == 0 else i * 16 + 32)
                            if g == 1 and b == 0:
                                high_next(eng, STAGE_C, i, p)
                        spread_k(i, p, g)
                        eng.wait_ge(c_pv, at4(i, p, g, 0, NT, NT + 4))
                        a.activation(osb[:], y_ps[g % 2][:], ACT.Copy).then_inc(c_osb, 1)
                        shifts(i, p, g)
                        if g == SG - 1:
                            eng.wait_ge(c_ot, at(0, i, p, 1, 1))
                            a.activation(ah, tr_ps[:], ACT.Copy).then_inc(c_ah, 1)
                    eng.wait_ge(c_wo, at(0, i, p, 1, 1))
                    a.activation(accT[:, p, :], cb_ps[:], ACT.Identity, bias=bo[:, 0:1]).then_inc(acc_ready, 1)

            eng.wait_ge(xT_done, STAGE_D * NB + 2)
            a.activation(xTh[:, 0, :], tr_ps[:], ACT.Copy).then_inc(xTh_ready, 1)
            with eng.Fori(0, NB // 2) as i:
                for p in range(2):
                    for c in range(CD):
                        eng.wait_ge(d_up, at(0, i, p, CD, c + 1))
                        eng.wait_ge(d_hl, at(0, i, p, CD, c + 1))
                        a.activation(hf[:, c % 2, :], hid_ps[c][:], ACT.Silu, bias=b1d[:, c:c + 1]).then_inc(d_hf, 1)
                        eng.wait_ge(d_hf, at(0, i, p, CD, c + 1 + 4))
                        eng.wait_ge(d_down, at(0, i, p, CD, c + 1))
                        a.activation(hh[:, c, :], hf[:, c % 2, :], ACT.Copy).then_inc(d_hh, 1)
                    high_next(eng, STAGE_D, i, p, 1)

        @block.tensor
        def _(eng):
            t = nc.tensor
            eng.sem_inc(a_down, HH)
            eng.sem_inc(b_down, HH)
            eng.sem_inc(c_pv, 4)
            eng.sem_inc(d_down, 4)

            def fwd():
                for k in range(NT):
                    ins = t.transpose(tr_ps[:, k * P:(k + 1) * P], xn[:, k * P:(k + 1) * P], ident[:])
                ins.then_inc(xT_done, 1)

            def back(p):
                for k in range(NT):
                    ins = t.transpose(tr_ps[:, k * P:(k + 1) * P], accT[:, p, k * P:(k + 1) * P], ident[:])
                ins.then_inc(back_done, 1)
            eng.wait_ge(consts, 1)
            eng.wait_ge(in_small, 16 * len(SMALL))
            for b in range(NB):
                eng.wait_ge(in_ctx[min(b, 1)], 16)
                src = X if b else ctxr[:, 0, :]
                for k in range(NT):
                    c = (b * NT + k) * EA
                    ins = t.matmul(cb_ps[:, c:c + EA], src[:, b * BT + k * P:b * BT + (k + 1) * P], wga[:],
                                   start=True, stop=True)
                ins.then_inc(logits_done, 1)
                if b == NB // 2 - 1:
                    eng.wait_ge(xn_ready, 1)
                    fwd()

            def comb_transpose(width, done):
                for k in range(NT):
                    ins = t.transpose(tr_ps[0:width, k * P:(k + 1) * P], comb[:, k * width:(k + 1) * width], ident[:])
                ins.then_inc(done, 1)
            eng.wait_ge(xTl_ready, 1)
            eng.wait_ge(comb_ready, 1)
            comb_transpose(2 * EA, combT_done)
            eng.wait_ge(selr, 1)

            def up(i, p, u, par):
                eng.wait_ge(a_hf, at(0, i, p, UA, u + 1))
                e, c = divmod(u % UA, CA)
                mm3(hid_ps[u % 4][:], w1h[:, e, c * P:(c + 1) * P], w1l[:, e, c * P:(c + 1) * P],
                    xTh[:, par, :], xTl[:, par, :]).then_inc(a_up, 1)
            for u in range(UP_AHEAD_A):
                up(0, 0, u, 0)
            with eng.Fori(0, NB // 2) as i:
                for p in range(2):
                    def down(u):
                        e, c = divmod(u, CA)
                        if c == 0:
                            eng.wait_ge(a_wy, at(0, i, p, EA, e + 1))
                        if c == LAST:
                            eng.wait_ge(a_hl_pool, at(0, i, p, EA, e + 1 + 1))
                        else:
                            eng.wait_ge(a_hl, at(0, i, p, UV, e * LAST + c + 1 + LAST))
                        mm3(y_ps[e % 2][:], w2h[:, e, c, :], w2l[:, e, c, :], hh[:, u % 4, :], hl[:, u % 4, :],
                            start=c == 0, stop=c == CA - 1).then_inc(a_down, 1)
                    for u in range(UA):
                        e, c = divmod(u, CA)
                        if u >= UP_AHEAD_A:
                            up(i, p, u, p)
                        if u >= DOWN_LAG:
                            down(u - DOWN_LAG)
                        if c == 0:
                            if e == 0:
                                eng.wait_ge(combT_ready, at(0, i, p, 1, 1))
                            eng.wait_ge(a_cbs, at(0, i, p, EA, e + 1))
                            t.matmul(cb_ps[:], sel[0:2 * EA, e, :], combT[0:2 * EA, p, :], start=True, stop=True).then_inc(a_cb, 1)
                        if u == 4:
                            eng.wait_ge(acc_ready, at(STAGE_A, i, p, 1, 1))
                            back(1 - p)
                        if u == 17:
                            eng.wait_ge(x_updated, at(STAGE_A, i, p, 1, 1))
                            eng.wait_ge(xn_ready, at(STAGE_A, i, p, 1, 2))
                            fwd()
                        if u == 25:
                            eng.wait_ge(xTl_ready, at(STAGE_A, i, p, 1, 2))
                            eng.wait_ge(comb_ready, at(0, i, p, 1, 2))
                            comb_transpose(2 * EA, combT_done)
                    for k in range(DOWN_LAG):
                        up(i, p, UA + k, 1 - p)
                        down(UA - DOWN_LAG + k)
            def router(p):
                for k in range(NT):
                    d = tr_ps[:, k * EB:(k + 1) * EB]
                    t.matmul(d, xTh[:, p, k * P:(k + 1) * P], wgbh[:], start=True, stop=False)
                    t.matmul(d, xTh[:, p, k * P:(k + 1) * P], wgbl[:], start=False, stop=False)
                    ins = t.matmul(d, xTl[:, p, k * P:(k + 1) * P], wgbh[:], start=False, stop=True)
                ins.then_inc(b_logits, 1)
            eng.wait_ge(combT_ready, NB + 1)
            eng.wait_ge(wgb_split, 1)
            router(0)
            eng.wait_ge(bcomb_ready, 1)
            comb_transpose(2 * EB, bcombT_done)
            eng.wait_ge(selr, 2)
            eng.wait_ge(raw_lo, NRAW1)

            def up(i, p, e, par):
                eng.wait_ge(b_sg, at(0, i, p, EB, e + 1))
                w = e % EB
                mm3(hid_ps[e % 2][:], bw1h[:, w, :], bw1l[:, w, :], xTh[:, par, :], xTl[:, par, :]).then_inc(b_up1, 1)
                eng.wait_ge(b_hf, at(0, i, p, EB, e + 1))
                mm3(hid_ps[2 + e % 2][:], bw3h[:, w, :], bw3l[:, w, :], xTh[:, par, :], xTl[:, par, :]).then_inc(b_up3, 1)
            for e in range(UP_AHEAD_B):
                up(0, 0, e, 0)
            with eng.Fori(0, NB // 2) as i:
                for p in range(2):
                    def down(e):
                        eng.wait_ge(b_hl, at(0, i, p, EB, e + 1 + HB))
                        mm3(y_ps[0][:], bw2h[:, e, :], bw2l[:, e, :], hh[:, e % 4, :], hl[:, e % 4, :],
                            start=False, stop=e == EB - 1).then_inc(b_down, 1)
                    for e in range(EB):
                        if e >= UP_AHEAD_B:
                            up(i, p, e, p)
                        if e == 0:
                            eng.wait_ge(bcombT_ready, at(0, i, p, 1, 1))
                        eng.wait_ge(b_hw, at(0, i, p, EB, e + 1))
                        t.matmul(weight_ps[e % 2][:], sel[:, e, :], combT[:, p, :], start=True, stop=True).then_inc(b_cb, 1)
                        if e >= DOWN_LAG:
                            down(e - DOWN_LAG)
                        if e == 1:
                            eng.wait_ge(acc_ready, at(STAGE_B, i, p, 1, 1))
                            back(1 - p)
                            t.matmul(y_ps[0][:], b2bh[:], combT[:, p, :], start=True, stop=False)
                            t.matmul(y_ps[0][:], b2bl[:], combT[:, p, :], start=False, stop=False)
                        if e == 5:
                            eng.wait_ge(x_updated, at(STAGE_B, i, p, 1, 1))
                            eng.wait_ge(xn_ready, at(STAGE_B, i, p, 1, 2))
                            fwd()
                        if e == 7:
                            eng.wait_ge(xTl_ready, at(STAGE_B, i, p, 1, 2))
                            router(1 - p)
                    for k in range(DOWN_LAG):
                        if k < UP_AHEAD_B:
                            up(i, p, EB + k, 1 - p)
                        down(EB - DOWN_LAG + k)
                        if k == 0:
                            eng.wait_ge(bcomb_ready, at(0, i, p, 1, 2))
                            comb_transpose(2 * EB, bcombT_done)

            eng.wait_ge(bcombT_ready, NB + 1)
            eng.wait_ge(dequant, 1)
            eng.wait_ge(b_hw, NB * EB + 2)
            for c in range(CD):
                ins = t.matmul(cb_ps[:, c:c + 1], raw[:, NRAW2 % 4, c * P:(c + 1) * P], beta[:], start=True, stop=True)
            ins.then_inc(beta_done, 1)

            def at4(i, p, g, ahead, per_step, count):
                return i * (2 * SG * per_step) + ((p * SG + g + ahead) * per_step + count)

            def project(i, p, g, which, par, bank=cb_ps):
                xh, xl = (ch[:, par, :], cl[:, par, :]) if which else (xTh[:, par, :], xTl[:, par, :])
                mm3(bank[:], wqkh[:, which, (g + 2) % SG, :], wqkl[:, which, (g + 2) % SG, :], xh, xl).then_inc(c_proj, 1)

            def project_values(par):
                for b in range(NT):
                    bs = slice(b * P, (b + 1) * P)
                    ins = mm3(cb_ps[:, bs], ch[:, par, bs], cl[:, par, bs], wvoh[:, 0, :], wvol[:, 0, :])
                ins.then_inc(c_vp, 1)

            def scores(i, p, g, b):
                eng.wait_ge(c_max, at4(i, p, g, 1, NT, b + 1))
                t.matmul(hid_ps[b % 2][:], ident16[:], maskq[:].rearrange("p i k -> p (i k)"), start=True, stop=False)
                t.matmul(hid_ps[b % 2][:], qp[:, (g + 1) % 2, b * P:(b + 1) * P], kdiag[(g + 1) % 2][:, b, :],
                         start=False, stop=True).then_inc(c_s1, 1)

            def shift_rows(i, p, g):
                eng.wait_ge(c_nm, at4(i, p, g, 1, 1, 1))
                for b in range(NT):
                    ins = t.transpose(tr_ps[0:2 * HG, b * P:(b + 1) * P], nmb[:, b, :], ident[:])
                ins.then_inc(c_nmt, 1)

            def scores_T(i, p, g, b):
                eng.wait_ge(c_exp, at4(i, p, g, 0, NT, b + 1))
                s2 = hid_ps[2 + b % 2]
                t.matmul(s2[:], ident16[:], maskk[:].rearrange("p i k -> p (i k)"), start=True, stop=False)
                for h in range(HG):
                    t.matmul(s2[:, h * P:(h + 1) * P], selm[:, h, :], nmT[:, g % 2, b * P:(b + 1) * P], start=False, stop=False)
                t.matmul(s2[:], kp[:, g % 4, b * P:(b + 1) * P], qdiag[g % 2][:, b, :], start=False, stop=True).then_inc(c_s2, 1)

            def both_scores(i, p, g, b):
                if b == 0:
                    eng.wait_ge(c_kd, at4(i, p, g, 1, 1, 1))
                    eng.wait_ge(c_kd_dve, at4(i, p, g, 1, 1, 1))
                scores(i, p, g, b)
                if b == 0:
                    eng.wait_ge(c_qd, at4(i, p, g, 0, 1, 1))
                    eng.wait_ge(c_nmT, at4(i, p, g, 0, 1, 1))
                scores_T(i, p, g, b)

            def weigh_values(i, p, g, b):
                eng.wait_ge(c_exp, at4(i, p, g, 0, NT, b + 1 + 2))
                for h in range(HG):
                    c = (b * NH + g * HG + h) * (HD + 1)
                    ins = t.matmul(y_ps[g % 2][32 * h:32 * h + 32, b * P:(b + 1) * P], vals[:, p, c:c + 32],
                                   prob[b][:, h * P:(h + 1) * P], start=True, stop=True)
                ins.then_inc(c_pv, 1)

            def to_rows(i, p, g):
                eng.wait_ge(c_osb, at4(i, p, g, 0, 1, 2))
                for b in range(NT):
                    ins = t.transpose(tr_ps[:, b * P:(b + 1) * P], osb[:, b * P:(b + 1) * P], ident[:])
                ins.then_inc(c_ott, 1)
            eng.wait_ge(dequant, 4)
            eng.wait_ge(raw_lo, NRAW)
            eng.wait_ge(xTl_ready, STAGE_C * NB + 1)
            eng.wait_ge(c_cl, 1)
            eng.wait_ge(acc_ready, STAGE_C * NB + 1)
            for g in (-2, -1):
                for which in range(2):
                    if (g, which) == (-1, 0):
                        eng.wait_ge(c_qk, 1)
                    project(0, 0, g, which, 0, y_ps[g % 2] if which else cb_ps)
            eng.wait_ge(c_qk, 4)
            project_values(0)
            eng.wait_ge(selr, 3)
            eng.wait_ge(c_kd, 1)
            eng.wait_ge(c_kd_dve, 1)
            eng.wait_ge(acc_ready, STAGE_C * NB + 1)
            for b in range(NT):
                scores(0, 0, -1, b)
            shift_rows(0, 0, -1)
            both_scores(0, 0, 0, 0)
            both_scores(0, 0, 0, 1)
            with eng.Fori(0, NB // 2) as i:
                for p in range(2):
                    for g in range(SG):
                        par = p if g < 2 else 1 - p
                        if g == 0:
                            eng.wait_ge(c_v, at(0, i, p, 1, 1))
                        for b in range(NT):
                            if g or b >= 2:
                                both_scores(i, p, g, b)
                            if b == 1:
                                eng.wait_ge(c_qk, at4(i, p, g, 2, 2, 0))
                            if b:
                                weigh_values(i, p, g, b - 1)
                            if g == 0 and b == 1:
                                eng.wait_ge(acc_ready, at(STAGE_C, i, p, 1, 1))
                                eng.wait_ge(c_al, at(0, i, p, 1, 1))
                                back(1 - p)
                            if g == 1 and b == 0:
                                eng.wait_ge(xn_ready, at(STAGE_C, i, p, 1, 2))
                                eng.wait_ge(c_nmT, at4(i, p, g, 0, 1, 1))
                                fwd()
                            if g and b == 2:
                                if g == 1:
                                    eng.wait_ge(xTl_ready, at(STAGE_C, i, p, 1, 2))
                                eng.wait_ge(c_nmT, at4(i, p, g, 0, 1, 1))
                                to_rows(i, p, g - 1)
                            if b == 1:
                                eng.wait_ge(c_qk, at4(i, p, g, 2, 2, 0))
                                if g == 2:
                                    eng.wait_ge(xTl_ready, at(STAGE_C, i, p, 1, 2))
                                    eng.wait_ge(c_cl, at(0, i, p, 1, 2))
                                if g == 3:
                                    eng.wait_ge(c_v, at(0, i, p, 1, 2))
                                project(i, p, g, 0, par)
                                eng.wait_ge(c_osb, at4(i, p, g, 0, 1, 1))
                                project(i, p, g, 1, par, y_ps[(g + 1) % 2])
                        weigh_values(i, p, g, NT - 1)
                        if g == 0:
                            eng.wait_ge(x_updated, at(STAGE_C, i, p, 1, 1))
                        else:
                            eng.wait_ge(c_norm, at4(i, p, g, 0, 1, 0))
                        shift_rows(i, p, g)
                        if g == 2:
                            eng.wait_ge(c_qk, at4(i, p, g, 2, 2, 2))
                            project_values(1 - p)
                    eng.wait_ge(c_nmT, at4(i, p, SG - 1, 1, 1, 1))
                    to_rows(i, p, SG - 1)
                    both_scores(i, p, SG, 0)
                    eng.wait_ge(c_norm, at4(i, p, SG - 1, 0, 1, 1))
                    for b in range(NT):
                        ins = t.transpose(tr_ps[:, b * P:(b + 1) * P], xn[:, b * P:(b + 1) * P], ident[:])
                    ins.then_inc(c_ot, 1)
                    both_scores(i, p, SG, 1)
                    eng.wait_ge(c_qk, at4(i, p, SG - 1, 2, 2, 2))
                    eng.wait_ge(c_al, at(0, i, p, 1, 2))
                    mm3(cb_ps[:], wvoh[:, 1, :], wvol[:, 1, :], ah, al).then_inc(c_wo, 1)

            eng.wait_ge(c_al, NB + 1)
            eng.wait_ge(xn_ready, STAGE_D * NB + 2)
            fwd()
            with eng.Fori(0, NB // 2) as i:
                for p in range(2):
                    def up(c):
                        eng.wait_ge(d_hf, at(0, i, p, CD, c + 1))
                        mm3(hid_ps[c][:], fc1h[:, c * P:(c + 1) * P], fc1l[:, c * P:(c + 1) * P],
                            xTh[:, p, :], xTl[:, p, :]).then_inc(d_up, 1)

                    def down(c):
                        eng.wait_ge(d_hl, at(0, i, p, CD, c + 1 + 2))
                        mm3(y_ps[p][:], fc2h[:, c, :], fc2l[:, c, :], hh[:, c, :], hl[:, c, :],
                            start=c == 0, stop=c == CD - 1).then_inc(d_down, 1)
                    eng.wait_ge(xTl_ready, at(STAGE_D, i, p, 1, 2))
                    up(0)
                    up(1)
                    eng.wait_ge(acc_ready, at(STAGE_D, i, p, 1, 1))
                    back(1 - p)
                    up(2)
                    up(3)
                    down(0)
                    down(1)
                    eng.wait_ge(x_updated, at(STAGE_D, i, p, 1, 1))
                    eng.wait_ge(xn_ready, at(STAGE_D, i, p, 1, 3))
                    fwd()
                    down(2)
                    down(3)
            eng.wait_ge(xTl_ready, NS * NB + 2)
            eng.wait_ge(acc_ready, NB * NS + 1)
            back(1)


SIGNS = np.zeros((P // 32, 4, HD, 2), np.float32)
SIGNS[:, 1, :, 0] = -1.0
SIGNS[:, 2, :, 1] = -1.0
SIGNS = SIGNS.reshape(P, 2)


def kernel(**inputs):
    import concourse.bacc as bacc
    from concourse.bass_utils import run_bass_kernel_spmd
    nc = bacc.Bacc("TRN2", target_bir_lowering=False, num_devices=1)
    g = {k: np.asarray(v) for k, v in inputs.items()}
    A, B, C, D = "L0_xattn_", "L0_ffn_", "L1_xattn_", "L1_ffn_"

    def head_rows(w):
        wt = w.T.reshape(P, NH, HD)
        return np.concatenate([wt, wt, wt, np.zeros_like(wt)], axis=2).reshape(P, -1)
    arrays = {
        "x": g["x"].reshape(-1, P),
        "ctxT": g["ctx_1024"].reshape(-1, P).T,
        "a_wg": g[A + "Wg"],
        "a_bg": np.broadcast_to(g[A + "bg"], (P, EA)),
        "a_w1": g[A + "W1"].transpose(1, 0, 2).reshape(P, -1),
        "a_b1": g[A + "b1"].reshape(-1, P).T,
        "a_w2": g[A + "W2"].reshape(EA, CA, P, P).transpose(2, 0, 1, 3).reshape(P, -1),
        "a_b2": g[A + "b2"].T,
        "b_wg": g[B + "Wg"].T,
        "b_w1": g[B + "W1"].transpose(2, 0, 1).reshape(P, -1),
        "b_b1": g[B + "b1"].T,
        "b_w3": g[B + "W3"].transpose(2, 0, 1).reshape(P, -1),
        "b_b3": g[B + "b3"].T,
        "b_w2": g[B + "W2"].transpose(2, 0, 1).reshape(P, -1),
        "b_b2": np.concatenate([g[B + "b2"], g[B + "b2"]], axis=0),
        "c_wqk": np.concatenate([head_rows(g[C + "Wq"]), head_rows(g[C + "Wk"])], axis=1),
        "c_wvo": np.concatenate([g[C + "Wv"].T, g[C + "Wo"].T], axis=1),
        "c_sign": SIGNS,
        "c_bv": np.broadcast_to(g[C + "bv"], (P, P)),
        "c_bo": g[C + "bo"].reshape(P, 1),
        "d_fc1": g[D + "fc1_q"],
        "d_fc2": g[D + "fc2_q"].reshape(CD, P, P).transpose(1, 0, 2).reshape(P, -1),
        "d_scales": np.concatenate([np.broadcast_to(g[D + "fc1_scales"].reshape(1, -1), (P, BT)),
                                    np.broadcast_to(g[D + "fc2_scales"].reshape(1, -1), (P, BT))], axis=1),
        "d_gamma": g[D + "ln_gamma"].reshape(P, 1),
        "d_beta": g[D + "ln_beta"].reshape(P, 1),
        "d_b1": g[D + "fc1_bias"].reshape(CD, P).T,
        "d_b2": g[D + "fc2_bias"].reshape(P, 1),
    }
    arrays = {k + "_in": np.ascontiguousarray(v) for k, v in arrays.items()}
    args = [nc.dram_tensor(k, v.shape, mybir.dt.from_np(v.dtype), kind="ExternalInput").ap() for k, v in arrays.items()]
    o = nc.dram_tensor("out", (NB * BT, P), F32, kind="ExternalOutput").ap()
    build(nc, *args, o)
    r = run_bass_kernel_spmd(nc, [arrays], core_ids=[0])
    return r.results[0]["out"].reshape(g["x"].shape)
```
